# Optimizing a Trainium2 kernel written in Bass

```python
import numpy as np
import jax
import jax.numpy as jnp

def _softmax(x, axis=-1):
    return jax.nn.softmax(x, axis=axis)

def _gelu(x):
    return jax.nn.gelu(x, approximate=True)

def _silu(x):
    return jax.nn.silu(x)

def _sigmoid(x):
    return jax.nn.sigmoid(x)

def _layernorm(x, axis=-1, eps=1e-05):
    m = jnp.mean(x, axis=axis, keepdims=True)
    v = jnp.var(x, axis=axis, keepdims=True)
    return (x - m) / jnp.sqrt(v + eps)

def _scatter_add(tgt, idx, src, axis=0):
    return tgt.at[idx].add(src)

def _segment_sum(src, seg, n):
    return jax.ops.segment_sum(src, seg, n)
kernel_name = 'mk_gnn_resnorm_d2_gnn_r32_79c749'

def setup_inputs(seed: int=0):
    np.random.seed(seed)
    _w = jnp.asarray

    def _rec_inputs():
        import jax
        import jax.numpy as jnp
        _gk = jax.random.key(seed)
        x = -0.000202 + 1 * jax.random.normal(jax.random.fold_in(_gk, 1), (50000, 128), jnp.float32)
        src = jax.random.randint(jax.random.fold_in(_gk, 2), (50000,), 0, 50000, jnp.int32)
        dst = jax.random.randint(jax.random.fold_in(_gk, 3), (50000,), 0, 50000, jnp.int32)
        _o = jnp.argsort(dst, stable=True)
        src = src[_o]
        dst = dst[_o]
        edge_attr_32 = 0.000254156 + 0.999948 * jax.random.normal(jax.random.fold_in(_gk, 11), (50000, 32), jnp.float32)
        return (x, src, dst, edge_attr_32)
    x, src, dst, edge_attr_32 = _rec_inputs()

    def _L0_gnn_setup():
        import jax, jax.numpy as jnp
        import numpy as np
        N, E = (50000, 12500)
        HID, EDIM, H, FFN_MULT = (128, 32, 2, 2)
        C = HID

        def _layernorm(x, g, b, eps=1e-05):
            mu = jnp.mean(x, axis=-1, keepdims=True)
            var = jnp.mean(jnp.square(x - mu), axis=-1, keepdims=True)
            return (x - mu) * jax.lax.rsqrt(var + eps) * g + b
        key = jax.random.key(seed)
        ks = jax.random.split(key, 16)
        s = 0.05
        inp = {'x': jax.random.normal(ks[0], (N, HID), jnp.float32), 'edge_index': jax.random.randint(ks[1], (2, E), 0, N, jnp.int64), 'edge_attr': jax.random.normal(ks[2], (E, EDIM), jnp.float32), 'Wq': jax.random.normal(ks[3], (H * C, HID), jnp.float32) * s, 'bq': jnp.zeros((H * C,), jnp.float32), 'Wk': jax.random.normal(ks[4], (H * C, HID), jnp.float32) * s, 'bk': jnp.zeros((H * C,), jnp.float32), 'Wv': jax.random.normal(ks[5], (H * C, HID), jnp.float32) * s, 'bv': jnp.zeros((H * C,), jnp.float32), 'We': jax.random.normal(ks[6], (H * C, EDIM), jnp.float32) * s, 'Wskip': jax.random.normal(ks[7], (HID, HID), jnp.float32) * s, 'bskip': jnp.zeros((HID,), jnp.float32), 'ln1_g': jnp.ones((HID,), jnp.float32), 'ln1_b': jnp.zeros((HID,), jnp.float32), 'W1': jax.random.normal(ks[8], (HID * FFN_MULT, HID), jnp.float32) * s, 'b1': jnp.zeros((HID * FFN_MULT,), jnp.float32), 'W2': jax.random.normal(ks[9], (HID, HID * FFN_MULT), jnp.float32) * s, 'b2': jnp.zeros((HID,), jnp.float32), 'ln2_g': jnp.ones((HID,), jnp.float32), 'ln2_b': jnp.zeros((HID,), jnp.float32)}
        return inp
    _L0_gnn_all = _L0_gnn_setup()
    _L0_gnn_in = {k: v for k, v in _L0_gnn_all.items() if k in ('Wq', 'bq', 'Wk', 'bk', 'Wv', 'bv', 'We', 'Wskip', 'bskip', 'ln1_g', 'ln1_b', 'W1', 'b1', 'W2', 'b2', 'ln2_g', 'ln2_b')}
    del _L0_gnn_all

    def _L1_gnn_setup():
        import jax, jax.numpy as jnp
        import numpy as np
        N, E, D, H, C = (50000, 25000, 128, 4, 32)
        NEG_SLOPE = 0.2
        LN_EPS = 1e-05
        NORM_EPS = 1e-12
        key = jax.random.key(seed)
        ks = jax.random.split(key, 10)
        s = 1.0 / np.sqrt(D)
        return {'x': jax.random.normal(ks[0], (N, D), dtype=jnp.float32), 'edge_index': jax.random.randint(ks[1], (2, E), 0, N, dtype=jnp.int64), 'gamma': 1.0 + 0.1 * jax.random.normal(ks[2], (D,), dtype=jnp.float32), 'beta': 0.1 * jax.random.normal(ks[3], (D,), dtype=jnp.float32), 'W_l': jax.random.normal(ks[4], (D, H * C), dtype=jnp.float32) * s, 'b_l': jnp.zeros((H * C,), dtype=jnp.float32), 'W_r': jax.random.normal(ks[5], (D, H * C), dtype=jnp.float32) * s, 'b_r': jnp.zeros((H * C,), dtype=jnp.float32), 'att': jax.random.normal(ks[6], (H, C), dtype=jnp.float32) * s, 'bias': jnp.zeros((H * C,), dtype=jnp.float32), 'scale': jnp.array(1.0, dtype=jnp.float32)}
    _L1_gnn_all = _L1_gnn_setup()
    _L1_gnn_in = {k: v for k, v in _L1_gnn_all.items() if k in ('gamma', 'beta', 'W_l', 'b_l', 'W_r', 'b_r', 'att', 'bias', 'scale')}
    del _L1_gnn_all
    return {'x': x, 'src': src, 'dst': dst, 'edge_attr_32': edge_attr_32, 'L0_gnn_Wq': _L0_gnn_in['Wq'], 'L0_gnn_bq': _L0_gnn_in['bq'], 'L0_gnn_Wk': _L0_gnn_in['Wk'], 'L0_gnn_bk': _L0_gnn_in['bk'], 'L0_gnn_Wv': _L0_gnn_in['Wv'], 'L0_gnn_bv': _L0_gnn_in['bv'], 'L0_gnn_We': _L0_gnn_in['We'], 'L0_gnn_Wskip': _L0_gnn_in['Wskip'], 'L0_gnn_bskip': _L0_gnn_in['bskip'], 'L0_gnn_ln1_g': _L0_gnn_in['ln1_g'], 'L0_gnn_ln1_b': _L0_gnn_in['ln1_b'], 'L0_gnn_W1': _L0_gnn_in['W1'], 'L0_gnn_b1': _L0_gnn_in['b1'], 'L0_gnn_W2': _L0_gnn_in['W2'], 'L0_gnn_b2': _L0_gnn_in['b2'], 'L0_gnn_ln2_g': _L0_gnn_in['ln2_g'], 'L0_gnn_ln2_b': _L0_gnn_in['ln2_b'], 'L1_gnn_gamma': _L1_gnn_in['gamma'], 'L1_gnn_beta': _L1_gnn_in['beta'], 'L1_gnn_W_l': _L1_gnn_in['W_l'], 'L1_gnn_b_l': _L1_gnn_in['b_l'], 'L1_gnn_W_r': _L1_gnn_in['W_r'], 'L1_gnn_b_r': _L1_gnn_in['b_r'], 'L1_gnn_att': _L1_gnn_in['att'], 'L1_gnn_bias': _L1_gnn_in['bias'], 'L1_gnn_scale': _L1_gnn_in['scale']}

def reference(x, src, dst, edge_attr_32, L0_gnn_Wq, L0_gnn_bq, L0_gnn_Wk, L0_gnn_bk, L0_gnn_Wv, L0_gnn_bv, L0_gnn_We, L0_gnn_Wskip, L0_gnn_bskip, L0_gnn_ln1_g, L0_gnn_ln1_b, L0_gnn_W1, L0_gnn_b1, L0_gnn_W2, L0_gnn_b2, L0_gnn_ln2_g, L0_gnn_ln2_b, L1_gnn_gamma, L1_gnn_beta, L1_gnn_W_l, L1_gnn_b_l, L1_gnn_W_r, L1_gnn_b_r, L1_gnn_att, L1_gnn_bias, L1_gnn_scale):
    import jax
    import jax.numpy as jnp

    def _L0_gnn_ref(x, edge_index, edge_attr, Wq, bq, Wk, bk, Wv, bv, We, Wskip, bskip, ln1_g, ln1_b, W1, b1, W2, b2, ln2_g, ln2_b):
        import jax, jax.numpy as jnp
        import numpy as np
        N, E = (50000, 12500)
        HID, EDIM, H, FFN_MULT = (128, 32, 2, 2)
        C = HID

        def _layernorm(x, g, b, eps=1e-05):
            mu = jnp.mean(x, axis=-1, keepdims=True)
            var = jnp.mean(jnp.square(x - mu), axis=-1, keepdims=True)
            return (x - mu) * jax.lax.rsqrt(var + eps) * g + b
        n = x.shape[0]
        src, dst = (edge_index[0], edge_index[1])
        q = (x @ Wq.T + bq).reshape(n, H, C)
        k = (x @ Wk.T + bk).reshape(n, H, C)
        v = (x @ Wv.T + bv).reshape(n, H, C)
        e = (edge_attr @ We.T).reshape(-1, H, C)
        k_j = k[src] + e
        alpha = jnp.sum(q[dst] * k_j, axis=-1) / jnp.sqrt(jnp.float32(C))
        amax = jax.ops.segment_max(alpha, dst, num_segments=n)
        amax = jnp.where(jnp.isfinite(amax), amax, 0.0)
        ex = jnp.exp(alpha - amax[dst])
        denom = jax.ops.segment_sum(ex, dst, num_segments=n)
        w = ex / (denom[dst] + 1e-16)
        msg = (v[src] + e) * w[:, :, None]
        agg = jax.ops.segment_sum(msg, dst, num_segments=n)
        out = jnp.mean(agg, axis=1)
        attn_out = out + x @ Wskip.T + bskip
        h = _layernorm(x + attn_out, ln1_g, ln1_b)
        f = jax.nn.leaky_relu(h @ W1.T + b1, negative_slope=0.01) @ W2.T + b2
        return _layernorm(h + f, ln2_g, ln2_b)

    def _L1_gnn_ref(x, edge_index, gamma, beta, W_l, b_l, W_r, b_r, att, bias, scale):
        import jax, jax.numpy as jnp
        import numpy as np
        N, E, D, H, C = (50000, 25000, 128, 4, 32)
        NEG_SLOPE = 0.2
        LN_EPS = 1e-05
        NORM_EPS = 1e-12
        n = x.shape[0]
        mu = jnp.mean(x, axis=-1, keepdims=True)
        var = jnp.mean(jnp.square(x - mu), axis=-1, keepdims=True)
        h = jax.nn.relu((x - mu) / jnp.sqrt(var + LN_EPS) * gamma + beta)
        loops = jnp.arange(n, dtype=edge_index.dtype)
        src = jnp.concatenate([edge_index[0], loops])
        dst = jnp.concatenate([edge_index[1], loops])
        xl = (h @ W_l + b_l).reshape(n, H, C)
        xr = (h @ W_r + b_r).reshape(n, H, C)
        feat = jax.nn.leaky_relu(xl[src] + xr[dst], NEG_SLOPE)
        e = jnp.einsum('ehc,hc->eh', feat, att)
        m = jax.ops.segment_max(e, dst, num_segments=n)
        p = jnp.exp(e - m[dst])
        denom = jax.ops.segment_sum(p, dst, num_segments=n)
        alpha = p / denom[dst]
        msg = alpha[:, :, None] * xl[src]
        out = jax.ops.segment_sum(msg, dst, num_segments=n).reshape(n, H * C) + bias
        out_norm = jnp.sqrt(jnp.sum(jnp.square(out), axis=-1, keepdims=True))
        msg_n = out / jnp.maximum(out_norm, NORM_EPS)
        h_norm = jnp.sqrt(jnp.sum(jnp.square(h), axis=-1, keepdims=True))
        gat_out = msg_n * h_norm * scale
        return x + gat_out
    edge_index = jnp.stack([src, dst])
    x = _layernorm(x + _L0_gnn_ref(x, edge_index, edge_attr_32, L0_gnn_Wq, L0_gnn_bq, L0_gnn_Wk, L0_gnn_bk, L0_gnn_Wv, L0_gnn_bv, L0_gnn_We, L0_gnn_Wskip, L0_gnn_bskip, L0_gnn_ln1_g, L0_gnn_ln1_b, L0_gnn_W1, L0_gnn_b1, L0_gnn_W2, L0_gnn_b2, L0_gnn_ln2_g, L0_gnn_ln2_b), axis=-1)
    x = _layernorm(x + _L1_gnn_ref(x, edge_index, L1_gnn_gamma, L1_gnn_beta, L1_gnn_W_l, L1_gnn_b_l, L1_gnn_W_r, L1_gnn_b_r, L1_gnn_att, L1_gnn_bias, L1_gnn_scale), axis=-1)
    return x

_drawn_inputs = setup_inputs


def setup_inputs(seed=0):
    import zlib

    import numpy as np

    out = dict(_drawn_inputs(seed))
    spreads = {'L0_gnn_bq': (0.0, 0.8),
     'L0_gnn_bk': (0.0, 0.8),
     'L0_gnn_bv': (0.0, 0.296),
     'L0_gnn_bskip': (0.0, 0.1),
     'L0_gnn_ln1_g': (1.0, 0.2),
     'L0_gnn_ln1_b': (0.0, 0.1),
     'L0_gnn_b1': (0.0, 0.293),
     'L0_gnn_b2': (0.0, 0.1),
     'L0_gnn_ln2_g': (1.0, 0.2),
     'L0_gnn_ln2_b': (0.0, 0.1),
     'L1_gnn_b_l': (0.0, 0.1),
     'L1_gnn_b_r': (0.0, 0.8),
     'L1_gnn_bias': (0.0, 0.1)}
    factors = {'L0_gnn_Wq': 3.389, 'L0_gnn_Wk': 3.714, 'L1_gnn_W_r': 5.3}
    for name, (base, spread) in spreads.items():
        noise = np.random.default_rng([zlib.crc32(name.encode()), seed]).standard_normal(out[name].shape)
        drawn = base * np.exp(spread * noise) if base else spread * noise
        out[name] = jnp.asarray(drawn.astype(out[name].dtype))
    for name, factor in factors.items():
        out[name] = (out[name] * factor).astype(out[name].dtype)
    return out
```

```python
from contextlib import ExitStack

import concourse.bass as bass
from concourse import mybir

F32 = mybir.dt.float32
I32 = mybir.dt.int32
U32 = mybir.dt.uint32
ALU = mybir.AluOpType
ACT = mybir.ActivationFunctionType
AX = mybir.AxisListType

P = 128
LANES = 4
W = P * LANES
N_NODES = 50000
BLOCKS = -(-N_NODES // W)
NP = BLOCKS * W
H0, H1 = 2, 4
C1 = P // H1
EDIM = 32
ROWS_E = H0 * EDIM + H0
DEN0 = H0 * EDIM
VCOL = P + 1
GROW = P + 2 * H1
SKIP = 1048576
FAR = -1e30
FILL = 14
EPS = 1e-5
HEAD = 3


class Phase:
    pass


def back(blk, lag):
    return blk[0], blk[1] - lag


def parity(blk):
    return blk[1] % 2


def at(blk, size):
    return blk[0] * (2 * size) + blk[1] * size


def static(blk):
    return isinstance(blk[0], int)


def total(blk, per_block):
    return at(blk, per_block) + per_block


def part(blk, per_block, done):
    return at(blk, per_block) + done


def slot(blk, per_block):
    return blk[0] * per_block + (blk[1] // 2 + 1) * per_block


def since(blk, lag):
    return not static(blk) or blk[1] >= lag


def steps(eng, lags, body):
    for s in range(2 * HEAD):
        body((0, s))
    with eng.Fori(HEAD, BLOCKS // 2) as i:
        for u in range(2):
            body((i, u))
    for s in range(BLOCKS, BLOCKS + lags):
        body((0, s))


def active(blk):
    return not static(blk) or 0 <= blk[1] < BLOCKS


def within(blk):
    return (0, min(blk[1], BLOCKS - 1)) if static(blk) else blk


def build(nc, t, out):
    ctx = ExitStack()
    with ctx:
        def sb(name, shape, dt=F32):
            return ctx.enter_context(nc.sbuf_tensor(name, shape, dt))

        def sem(name):
            return ctx.enter_context(nc.semaphore(name))

        def sem2(name):
            return [sem(f"{name}_{k}") for k in range(2)]

        reset_d = nc.dram_tensor("reset_d", (BLOCKS, W), F32, kind="Internal").ap()
        agg_d = nc.dram_tensor("agg_d", (NP, P), F32, kind="Internal").ap()
        x1_d = nc.dram_tensor("x1_d", (NP, P), F32, kind="Internal").ap()
        xl_d = nc.dram_tensor("xl_d", (NP, P), F32, kind="Internal").ap()
        xr_d = nc.dram_tensor("xr_d", (NP, P), F32, kind="Internal").ap()
        gat_d = nc.dram_tensor("gat_d", (NP, GROW), F32, kind="Internal").ap()

        ident = sb("ident", [P, P])
        wq = sb("wq", [P, H0, P])
        wk = sb("wk", [P, H0, P])
        wexb = sb("wexb", [P, H0, ROWS_E])
        bq = sb("bq", [P, H0])
        qk = sb("qk", [P, H0, P])
        qe = sb("qe", [P, ROWS_E])
        ck = sb("ck", [P, H0])
        ce = sb("ce", [ROWS_E, 1])
        sumx = sb("sumx", [P, H0, ROWS_E])
        sume = sb("sume", [ROWS_E, ROWS_E])
        spread_w = sb("spread_w", [ROWS_E, H0, P])
        wv = sb("wv", [P, H0, P])
        wve = sb("wve", [ROWS_E, H0, VCOL])
        wskip = sb("wskip", [P, P])
        w1 = sb("w1", [P, 2, P])
        w2 = sb("w2", [P, 2, P])
        wlr = sb("wlr", [P, 2, P])
        cols = sb("cols", [P, 8])
        b1s = sb("b1s", [P, 2])
        rows = sb("rows", [P, 7, P])
        attb = sb("attb", [P, P])
        headmask = sb("headmask", [P, P])
        headpick = sb("headpick", [P, H1])
        ones = sb("ones", [P, 1])
        epsc = sb("epsc", [P, 1])
        scalec = sb("scalec", [P, 1])
        hnorm = sb("hnorm", [P, BLOCKS, LANES])
        fill = sb("fill", [P, FILL, GROW])
        zeros = sb("zeros", [P, FILL, P])
        dstrow = sb("dstrow", [BLOCKS, 2, W], I32)
        resets = sb("resets", [BLOCKS, W])

        ARENA = 46
        arena = sb("arena", [P, ARENA, W + 4])
        taken = [0]

        def phase_tiles():
            taken[0] = 0

        def tile(parts=P, width=W):
            k = taken[0]
            n = -(-width // (W + 4))
            taken[0] += n
            assert taken[0] <= ARENA, taken
            return arena[0:parts, k:k + n, :].rearrange("p a w -> p (a w)")[:, 0:width]

        def tile2(parts=P, width=W):
            return [tile(parts, width) for _ in range(2)]

        def lanes(ap):
            return ap.rearrange("p (j f) -> p j f", j=LANES)

        bank = [ctx.enter_context(nc.psum_tensor(f"bank{k}", [P, W], F32)) for k in range(8)]

        idx = [sb(f"idx{k}", [P, 2, LANES], I32) for k in range(2)]
        ends = [sb(f"ends{k}", [P, 2, LANES], I32) for k in range(2)]
        lastf = sb("lastf", [P, LANES])
        last = [sb(f"last{k}", [P, LANES], I32) for k in range(2)]

        loaded = sem("weights_loaded")
        memset_done = sem("memset_done")
        prep_mm = sem("prep_products")
        prep_dve = sem("prep_vector")
        resets_done = sem("resets_computed")
        reset_stored = sem("resets_stored")
        filled = sem("tables_filled")
        hnorm_ready = sem("hnorm_ready")

        a = Phase()
        phase_tiles()
        a.xs, a.xd = tile2(), tile2()
        a.xsT, a.xdT = tile2(), tile2()
        a.ext, a.reset = tile2(ROWS_E), tile2(ROWS_E)
        a.prod = [tile(), tile()]
        a.prode = tile(ROWS_E)
        a.runmax = tile(ROWS_E, 2 * W + 1)
        a.shift = tile(ROWS_E, 2 * W)
        a.pd = [tile(ROWS_E, 2 * W), tile(ROWS_E, 2 * W)]
        a.pv = [tile(), tile()]
        a.pve = tile(ROWS_E)
        a.num = [tile2(), tile2()]
        a.nume = tile2(ROWS_E)
        a.agg = tile2()
        a.den = [sb(f"a_den{k}", [P, H0]) for k in range(2)]
        a.rden = [sb(f"a_rden{k}", [P, H0]) for k in range(2)]
        a.turned = sem("a_turned")
        a.evacuated = sem("a_evacuated")
        a.projected = sem("a_projected")
        a.products = sem("a_products")
        a.scored = sem("a_scored")
        a.maxima = sem("a_maxima")
        a.shifts = sem("a_shifts")
        a.weights = sem("a_weights")
        a.spread = sem("a_spread")
        a.weighted = sem("a_weighted")
        a.summed = sem("a_summed")
        a.values = sem("a_values")
        a.denoms = sem("a_denoms")
        a.head0 = sem("a_head0")
        a.combined = sem("a_combined")
        a.carried = sem("a_carried")
        a.lastrow = sem("a_lastrow")
        a.go = sem("a_go")
        a.idx_in = sem2("a_idx_in")
        a.ends_in = sem2("a_ends_in")
        a.edge_in = sem2("a_edge_in")
        a.gathered = sem2("a_gathered")
        a.scattered = sem2("a_scattered")

        c = Phase()
        phase_tiles()
        c.xl, c.xr = tile2(), tile2()
        c.xlT = tile2()
        c.reset = tile2()
        c.z, c.leaky = tile(), tile()
        c.runmax = tile(P, 2 * W + 1)
        c.shift = tile(P, 2 * W)
        c.pd = [tile(P, 2 * W), tile(P, 2 * W)]
        c.pv = tile()
        c.num, c.den = tile2(), tile2()
        c.row = [tile(P, LANES * GROW), tile(P, LANES * GROW)]
        c.turned = sem("c_turned")
        c.evacuated = sem("c_evacuated")
        c.feats = sem("c_feats")
        c.scored = sem("c_scored")
        c.maxima = sem("c_maxima")
        c.shifts = sem("c_shifts")
        c.weights = sem("c_weights")
        c.weighted = sem("c_weighted")
        c.summed = sem("c_summed")
        c.returned = sem("c_returned")
        c.packed = sem("c_packed")
        c.carried = sem("c_carried")
        c.lastrow = sem("c_lastrow")
        c.go = sem("c_go")
        c.idx_in = sem2("c_idx_in")
        c.ends_in = sem2("c_ends_in")
        c.edge_in = sem2("c_edge_in")
        c.gathered = sem2("c_gathered")
        c.scattered = sem2("c_scattered")

        def stats_tiles(name):
            q = Phase()
            q.stats = sb(name + "_stats", [P, LANES, 6])
            q.mv = sb(name + "_mv", [P, LANES, 2])
            q.sd = sb(name + "_sd", [P, LANES])
            q.rstd = sb(name + "_rstd", [P, LANES])
            q.nbias = sb(name + "_nbias", [P, LANES])
            q.moments, q.root, q.ready, q.applied, q.go = (
                sem(f"{name}_{n}") for n in ("moments", "root", "ready", "applied", "go"))
            return q

        b = Phase()
        phase_tiles()
        b.x, b.xT, b.agg = tile2(), tile2(), tile2()
        b.y, b.z = tile(), tile()
        b.hT = tile2()
        b.small = [tile(), tile()]
        b.f = [tile(), tile()]
        b.y2T = tile()
        b.xb = tile2()
        b.z2 = tile()
        b.y3 = tile2()
        b.x1 = tile2()
        b.z4 = tile()
        b.h1T = tile()
        b.sq = tile()
        b.xl, b.xr = tile2(), tile2()
        b.ln = [stats_tiles(f"b_ln{k}") for k in range(4)]
        b.resid = sem("b_resid")
        b.skipped = sem("b_skipped")
        b.y_ready = sem("b_y_ready")
        b.turned1 = sem("b_turned1")
        b.h_ready = sem("b_h_ready")
        b.up = sem("b_up")
        b.small_up = sem("b_small_up")
        b.act_up = sem("b_act_up")
        b.down = sem("b_down")
        b.y2_ready = sem("b_y2_ready")
        b.turned2 = sem("b_turned2")
        b.y3_ready = sem("b_y3_ready")
        b.turned4 = sem("b_turned4")
        b.h1_ready = sem("b_h1_ready")
        b.squared = sem("b_squared")
        b.normed = sem("b_normed")
        b.lr = sem("b_lr")
        b.lr_ready = sem("b_lr_ready")
        b.hn_saved = sem("b_hn_saved")
        b.node_in = sem2("b_node_in")
        b.xb_in = sem2("b_xb_in")
        b.x1_out = sem2("b_x1_out")
        b.lr_out = sem2("b_lr_out")

        d = Phase()
        phase_tiles()
        d.x1, d.xl, d.xr = tile2(), tile2(), tile2()
        d.g = [tile(P, LANES * GROW), tile(P, LANES * GROW)]
        d.z, d.lk = tile(), tile()
        d.o, d.o2 = tile(), tile()
        d.sq = tile()
        d.y = tile2()
        d.res = tile2()
        d.self_s = sb("d_self", [P, LANES * H1])
        d.top = sb("d_top", [P, LANES * H1])
        d.ex = [sb(f"d_ex{k}", [P, 2, LANES * H1]) for k in range(2)]
        d.diff = sb("d_diff", [P, 2, LANES * H1])
        d.dn = sb("d_dn", [P, LANES * H1])
        d.ss = sb("d_ss", [P, LANES])
        d.nrm = sb("d_nrm", [P, LANES])
        d.fac = sb("d_fac", [P, LANES])
        d.ln = stats_tiles("d_ln")
        d.z_ready = sem("d_z_ready")
        d.doubled = sem("d_doubled")
        d.lk_ready = sem("d_lk_ready")
        d.la_ready = sem("d_la_ready")
        d.self_ready = sem("d_self_ready")
        d.top_ready = sem("d_top_ready")
        d.diffs = sem("d_diffs")
        d.exps = sem("d_exps")
        d.shares = sem("d_shares")
        d.part_e = sem("d_part_e")
        d.part_s = sem("d_part_s")
        d.sum_es = sem("d_sum_es")
        d.o_ready = sem("d_o_ready")
        d.sq_ready = sem("d_sq_ready")
        d.nrm_ready = sem("d_nrm_ready")
        d.fac_ready = sem("d_fac_ready")
        d.y_ready = sem("d_y_ready")
        d.node_in = sem2("d_node_in")
        d.out_done = sem2("d_out_done")

        def wait_prep(eng):
            eng.wait_ge(loaded, 16 * N_LOADS)
            eng.wait_ge(memset_done, 8)
            eng.wait_ge(prep_dve, 9)

        def wait_filled(eng):
            eng.wait_ge(filled, 16 * 2 * (NP // (FILL * P)))

        def wait_scatters(eng, q):
            for k in range(2):
                eng.wait_ge(q.scattered[k], 16 * LANES * BLOCKS // 2)

        def wait_node_stores(eng):
            for k in range(2):
                eng.wait_ge(b.x1_out[k], 16 * BLOCKS // 2)
                eng.wait_ge(b.lr_out[k], 32 * BLOCKS // 2)

        def heads(ap):
            return ap.rearrange("p (h e) -> p h e", e=C1)

        def wide(ap):
            return ap.unsqueeze(2).to_broadcast([P, LANES * H1, C1])

        def gsum(ap):
            return ap.rearrange("p (j f) -> p j f", j=LANES)[:, :, 0:P].rearrange("p j (h e) -> p j h e", e=C1)

        loads = [
            (ident[:, :], t["ident"]), (headmask[:, :], t["headmask"]), (headpick[:, :], t["headpick"]),
            (sumx[:, :, :], t["sumx"]), (sume[:, :], t["sume"]), (spread_w[:, :, :], t["spread_w"]),
            (wq[:, :, :], t["Wq"].rearrange("(h c) f -> c h f", h=H0)),
            (wk[:, :, :], t["Wk"].rearrange("(h c) f -> c h f", h=H0)),
            (wexb[:, :, :], t["wexb"]),
            (bq[:, :], t["bq"]),
            (wv[:, :, :], t["WvT"].rearrange("f (h c) -> f h c", h=H0)),
            (wve[:, :, :], t["wve"]),
            (wskip[:, :], t["WskipT"]),
            (w1[:, :, :], t["W1T"].rearrange("f (h c) -> f h c", h=2)),
            (w2[:, :, :], t["W2T"].rearrange("(h c) f -> c h f", h=2)),
            (wlr[:, 0, :], t["W_l"]), (wlr[:, 1, :], t["W_r"]),
            (cols[:, :], t["cols"]),
            (rows[:, :, :], t["rows"].partition_broadcast(P)),
            (scalec[:, :], t["scale"].partition_broadcast(P)),
            (dstrow[:, :, :], t["dstrow"]),
        ]
        N_LOADS = len(loads)

        block = ctx.enter_context(nc.Block())

        @block.sync
        def _(eng):
            for dst, src in loads:
                eng.dma_start(dst, src).then_inc(loaded, 16)
            eng.wait_ge(memset_done, 8)
            for k in range(NP // (FILL * P)):
                r = slice(k * FILL * P, (k + 1) * FILL * P)
                eng.dma_start(agg_d[r, :].rearrange("(p r) f -> p r f", p=P), zeros[:, :, :]).then_inc(filled, 16)
                eng.dma_start(gat_d[r, :].rearrange("(p r) f -> p r f", p=P), fill[:, :, :]).then_inc(filled, 16)
            eng.wait_ge(resets_done, 2)
            eng.dma_start(reset_d[:, :], resets[:, :]).then_inc(reset_stored, 16)
            eng.wait_ge(reset_stored, 16)

            def edge_indices(q, s):
                if active(s):
                    k = parity(s)
                    if since(s, 2):
                        eng.wait_ge(q.gathered[parity(back(s, 2))], slot(back(s, 2), 2 * 16 * LANES))
                    eng.dma_start(idx[k][:, :, :], t["idx"][bass.ds(at(s, 1), 1), :, 0:2, :].rearrange("a p v j -> (a p) v j")).then_inc(q.idx_in[k], 16)
                g = back(s, 2)
                if active(g):
                    k = parity(g)
                    if since(g, 2):
                        eng.wait_ge(q.lastrow, total(back(g, 2), 2))
                    eng.dma_start(ends[k][:, :, :], t["idx"][bass.ds(at(g, 1), 1), :, 1:3, :].rearrange("a p v j -> (a p) v j")).then_inc(q.ends_in[k], 16)

            def a_step(s):
                edge_indices(a, s)
                g = back(s, 1)
                if active(g):
                    k = parity(g)
                    if since(g, 2):
                        eng.wait_ge(a.shifts, total(back(g, 2), 3))
                    if since(g, 2):
                        eng.wait_ge(a.weighted, total(back(g, 2), 3))
                    eng.dma_start(a.reset[k], reset_d[bass.ds(at(g, 1), 1), :].partition_broadcast(ROWS_E)).then_inc(a.edge_in[k], 16)
                    for h in range(H0):
                        eng.dma_start(a.ext[k][h * EDIM:(h + 1) * EDIM, :], t["eaT"][:, bass.ds(at(g, W), W)]).then_inc(a.edge_in[k], 16)
            steps(eng, A_LAGS, a_step)

            wait_scatters(eng, a)

            def b_step(s):
                if active(s):
                    k = parity(s)
                    if since(s, 2):
                        eng.wait_ge(b.resid, total(back(s, 2), 2))
                    if since(s, 2):
                        eng.wait_ge(b.skipped, total(back(s, 2), 1))
                    if since(s, 2):
                        eng.wait_ge(b.y_ready, total(back(s, 2), 1))
                    r = bass.ds(at(s, W), W)
                    eng.dma_start(b.x[k], t["x"][r, :].rearrange("(p j) f -> p (j f)", p=P)).then_inc(b.node_in[k], 16)
                    eng.dma_start(b.xT[k], t["xT"][:, r]).then_inc(b.node_in[k], 16)
                    eng.dma_start(b.agg[k], agg_d[r, :].rearrange("(p j) f -> p (j f)", p=P)).then_inc(b.node_in[k], 16)
                g = back(s, 2)
                if active(g):
                    k = parity(g)
                    if since(g, 2):
                        eng.wait_ge(b.y3_ready, total(back(g, 2), 3))
                    eng.dma_start(b.xb[k], t["x"][bass.ds(at(g, W), W), :].rearrange("(p j) f -> p (j f)", p=P)).then_inc(b.xb_in[k], 16)
                g = back(s, 3)
                if active(g):
                    k = parity(g)
                    eng.wait_ge(b.ln[2].applied, total(g, LANES))
                    eng.dma_start(x1_d[bass.ds(at(g, W), W), :].rearrange("(p j) f -> p (j f)", p=P), b.x1[k]).then_inc(b.x1_out[k], 16)
                g = back(s, 4)
                if active(g):
                    k = parity(g)
                    r = bass.ds(at(g, W), W)
                    eng.wait_ge(b.lr_ready, total(g, 2))
                    eng.dma_start(xl_d[r, :].rearrange("(p j) f -> p (j f)", p=P), b.xl[k]).then_inc(b.lr_out[k], 16)
                    eng.dma_start(xr_d[r, :].rearrange("(p j) f -> p (j f)", p=P), b.xr[k]).then_inc(b.lr_out[k], 16)
            steps(eng, B_LAGS, b_step)

            wait_node_stores(eng)

            def c_step(s):
                edge_indices(c, s)
                g = back(s, 1)
                if active(g):
                    k = parity(g)
                    if since(g, 2):
                        eng.wait_ge(c.shifts, total(back(g, 2), 3))
                    eng.dma_start(c.reset[k], reset_d[bass.ds(at(g, 1), 1), :].partition_broadcast(P)).then_inc(c.edge_in[k], 16)
            steps(eng, A_LAGS, c_step)

            wait_scatters(eng, c)

            def d_step(s):
                if active(s):
                    k = parity(s)
                    g = back(s, 2)
                    if active(g):
                        eng.wait_ge(d.z_ready, total(g, 1))
                        eng.wait_ge(d.part_s, total(g, 1))
                        eng.wait_ge(d.part_e, total(g, 1))
                        eng.wait_ge(d.y_ready, total(g, LANES))
                    r = bass.ds(at(s, W), W)
                    for dst, src in ((d.x1[k], x1_d), (d.xl[k], xl_d), (d.xr[k], xr_d), (d.g[k], gat_d)):
                        eng.dma_start(dst, src[r, :].rearrange("(p j) f -> p (j f)", p=P)).then_inc(d.node_in[k], 16)
                g = back(s, 3)
                if active(g):
                    k = parity(g)
                    eng.wait_ge(d.ln.applied, total(g, LANES))
                    eng.dma_start(out[bass.ds(at(g, W), W), :].rearrange("(p j) f -> p (j f)", p=P), d.res[k]).then_inc(d.out_done[k], 16)
            steps(eng, D_LAGS, d_step)
            for k in range(2):
                eng.wait_ge(d.out_done[k], 16 * BLOCKS // 2)

        @block.gpsimd
        def _(eng):
            wait_prep(eng)
            wait_filled(eng)

            def edge_step(q, tab_s, tab_d, buf_s, buf_d, node_table, row_buf, row_width, s):
                if active(s):
                    k = parity(s)
                    eng.wait_ge(q.idx_in[parity(s)], slot(s, 16))
                    if since(s, 2):
                        eng.wait_ge(q.turned, total(back(s, 2), 2))
                    eng.sem_inc(q.go, 1)
                    for tab, buf, v in ((tab_s, buf_s, 0), (tab_d, buf_d, 1)):
                        for j in range(LANES):
                            eng.indirect_dma_start(
                                buf[k][:, j * P:(j + 1) * P], None, tab[:, :],
                                bass.IndirectOffsetOnAxis(ap=idx[k][:, v, j:j + 1].bitcast(U32), axis=0),
                            ).then_inc(q.gathered[k], 16)
                g = back(s, 4)
                if active(g):
                    k = parity(g)
                    eng.wait_ge(q.done_rows, total(g, q.rows_per_block))
                    eng.wait_ge(q.lastrow, total(g, 2))
                    eng.sem_inc(q.go, 1)
                    for j in range(LANES):
                        eng.indirect_dma_start(
                            node_table[:, :],
                            bass.IndirectOffsetOnAxis(ap=last4[parity4(g)][:, j:j + 1].bitcast(U32), axis=0),
                            row_buf[k][:, j * row_width:(j + 1) * row_width], None,
                            bounds_check=NP - 1, oob_is_err=False,
                        ).then_inc(q.scattered[k], 16)

            last4, parity4 = last, parity
            a.done_rows, a.rows_per_block = a.combined, LANES
            steps(eng, A_LAGS, lambda s: edge_step(a, t["x"], t["x"], a.xs, a.xd, agg_d, a.agg, P, s))
            for k in range(2):
                eng.wait_ge(a.scattered[k], 16 * LANES * BLOCKS // 2)

            def b_step(s):
                g = back(s, 1)
                if active(g):
                    k = parity(g)
                    eng.wait_ge(b.node_in[parity(g)], slot(g, 48))
                    eng.tensor_tensor(lanes(b.agg[k]), lanes(b.agg[k]), rows[:, 0:1, :].to_broadcast([P, LANES, P]), ALU.add).then_inc(b.resid, 1)
                    eng.wait_ge(b.resid, part(g, 2, 1))
                    eng.tensor_tensor(b.agg[k], b.agg[k], b.x[k], ALU.add).then_inc(b.resid, 1)
                g = back(s, 3)
                if active(g):
                    k = parity(g)
                    eng.wait_ge(b.ln[1].applied, total(g, LANES))
                    eng.wait_ge(b.xb_in[parity(g)], slot(g, 16))
                    if since(g, 2):
                        eng.wait_ge(b.ln[2].applied, total(back(g, 2), LANES))
                    eng.tensor_tensor(lanes(b.y3[k]), lanes(b.z2), rows[:, 1:2, :].to_broadcast([P, LANES, P]), ALU.mult).then_inc(b.y3_ready, 1)
                    eng.tensor_tensor(lanes(b.xb[k]), lanes(b.xb[k]), rows[:, 2:3, :].to_broadcast([P, LANES, P]), ALU.add).then_inc(b.y3_ready, 1)
                    eng.wait_ge(b.y3_ready, part(g, 3, 2))
                    eng.tensor_tensor(b.y3[k], b.y3[k], b.xb[k], ALU.add).then_inc(b.y3_ready, 1)
            steps(eng, B_LAGS, b_step)
            wait_node_stores(eng)

            c.done_rows, c.rows_per_block = c.packed, 2
            steps(eng, A_LAGS, lambda s: edge_step(c, xl_d, xr_d, c.xl, c.xr, gat_d, c.row, GROW, s))
            wait_scatters(eng, c)

            def d_step(s):
                g = back(s, 1)
                if active(g):
                    k = parity(g)
                    eng.wait_ge(d.node_in[parity(g)], slot(g, 64))
                    if since(g, 1):
                        eng.wait_ge(d.lk_ready, total(back(g, 1), 1))
                    eng.tensor_tensor(d.z, d.xl[k], d.xr[k], ALU.add).then_inc(d.z_ready, 1)
                    eng.tensor_tensor(d.x1[k], d.x1[k], d.x1[k], ALU.add).then_inc(d.doubled, 1)
                    eng.wait_ge(d.lk_ready, total(g, 1))
                    eng.tensor_tensor(lanes(d.lk), lanes(d.lk), rows[:, 5:6, :].to_broadcast([P, LANES, P]), ALU.mult).then_inc(d.la_ready, 1)
                g = back(s, 2)
                if active(g):
                    k = parity(g)
                    eng.wait_ge(d.shares, total(g, 4))
                    eng.tensor_tensor(heads(d.o), gsum(d.g[k]), wide(d.ex[k][:, 0, :]), ALU.mult).then_inc(d.part_e, 1)
                    eng.wait_ge(d.sum_es, total(g, 1))
                    eng.tensor_tensor(lanes(d.o2), lanes(d.o2), rows[:, 6:7, :].to_broadcast([P, LANES, P]), ALU.add).then_inc(d.o_ready, 1)
            steps(eng, D_LAGS, d_step)

        def norm_vector(eng, ln, src, g):
            for j in range(LANES):
                eng.bn_stats(ln.stats[:, j, :], src[:, j * P:(j + 1) * P]).then_inc(ln.moments, 1)
            eng.wait_ge(ln.moments, part(g, 2 * LANES, LANES))
            if since(g, 1):
                eng.wait_ge(ln.root, total(back(g, 1), 1))
            eng.sem_inc(ln.go, 1)
            for j in range(LANES):
                eng.bn_aggr(ln.mv[:, j, :], ln.stats[:, j, :]).then_inc(ln.moments, 1)
            eng.wait_ge(ln.root, total(g, 1))
            if since(g, 1):
                eng.wait_ge(ln.applied, total(back(g, 1), LANES))
            eng.wait_ge(ln.moments, total(g, 2 * LANES))
            eng.reciprocal(ln.rstd[:, :], ln.sd[:, :]).then_inc(ln.ready, 1)
            eng.wait_ge(ln.ready, part(g, 2, 1))
            eng.scalar_tensor_tensor(out=ln.nbias[:, :], in0=ln.mv[:, :, 0], scalar=-1.0, in1=ln.rstd[:, :],
                                     op0=ALU.mult, op1=ALU.mult).then_inc(ln.ready, 1)

        def norm_scalar(eng, ln, src, dst, g):
            eng.wait_ge(ln.moments, total(g, 2 * LANES))
            if since(g, 1):
                eng.wait_ge(ln.ready, total(back(g, 1), 2))
            eng.activation(ln.sd[:, :], ln.mv[:, :, 1], ACT.Sqrt, bias=epsc[:, 0:1]).then_inc(ln.root, 1)
            eng.wait_ge(ln.ready, total(g, 2))
            for j in range(LANES):
                eng.activation(dst[:, j * P:(j + 1) * P], src[:, j * P:(j + 1) * P], ACT.Identity,
                               bias=ln.nbias[:, j:j + 1], scale=ln.rstd[:, j:j + 1]).then_inc(ln.applied, 1)

        def find_last(eng, q, g):
            k = parity(g)
            eng.wait_ge(q.ends_in[parity(g)], slot(g, 16))
            if since(g, 1):
                eng.wait_ge(q.lastrow, total(back(g, 1), 2))
            if since(g, 2):
                eng.wait_ge(q.scattered[parity(back(g, 2))], slot(back(g, 2), 16 * LANES))
            eng.tensor_tensor(lastf[:, :], ends[k][:, 0, :], ends[k][:, 1, :], ALU.is_equal).then_inc(q.lastrow, 1)
            eng.wait_ge(q.lastrow, part(g, 2, 1))
            eng.scalar_tensor_tensor(out=last[k][:, :], in0=lastf[:, :], scalar=float(SKIP), in1=ends[k][:, 0, :],
                                     op0=ALU.mult, op1=ALU.add).then_inc(q.lastrow, 1)

        def run_maxima(eng, q, score, n, g):
            k = parity(g)
            o = k * W
            if k == 0:
                if since(g, 1):
                    eng.wait_ge(q.maxima, total(back(g, 1), 1))
                q.free_maxima(eng, g)
                eng.tensor_copy(q.runmax[:, 0:1], q.runmax[:, 2 * W:2 * W + 1]).then_inc(q.carried, 1)
                eng.wait_ge(q.carried, g[0] + g[1] // 2 + 1)
            eng.wait_ge(q.scored, total(g, q.scores_per_block))
            eng.wait_ge(q.edge_in[parity(g)], slot(g, q.edge_loads))
            if since(g, 1):
                eng.wait_ge(q.maxima, total(back(g, 1), 1))
            if since(g, 1):
                eng.wait_ge(q.shifts, total(back(g, 1), 3))
            if k == 1:
                q.free_maxima(eng, g)
            eng.tensor_tensor_scan(q.runmax[:, o + 1:o + W + 1], q.reset[k], score, q.runmax[:, o:o + 1],
                                   ALU.add, ALU.max).then_inc(q.maxima, 1)
            eng.wait_ge(q.maxima, total(g, 1))
            if since(g, 1):
                eng.wait_ge(q.weights, total(back(g, 1), 1))
            eng.tensor_tensor(q.shift[:, 0:W], score, q.runmax[:, o + 1:o + W + 1], ALU.subtract).then_inc(q.shifts, 1)
            eng.tensor_tensor(q.shift[:, W:2 * W], q.runmax[:, o:o + W], q.runmax[:, o + 1:o + W + 1], ALU.subtract).then_inc(q.shifts, 1)
            eng.wait_ge(q.shifts, part(g, 3, 2))
            eng.tensor_tensor(q.shift[:, W:2 * W], q.shift[:, W:2 * W], q.reset[k], ALU.add).then_inc(q.shifts, 1)

        @block.vector
        def _(eng):
            eng.memset(zeros[:, :, :], 0.0).then_inc(memset_done, 1)
            eng.memset(fill[:, :, 0:P + H1], 0.0).then_inc(memset_done, 1)
            eng.memset(fill[:, :, P + H1:GROW], FAR).then_inc(memset_done, 1)
            eng.memset(ones[:, :], 1.0).then_inc(memset_done, 1)
            eng.memset(epsc[:, :], EPS).then_inc(memset_done, 1)
            for k in range(2):
                eng.memset(a.ext[k][DEN0:ROWS_E, :], 1.0).then_inc(memset_done, 1)
            eng.memset(a.runmax[:, :], 0.0).then_inc(memset_done, 1)
            eng.wait_ge(loaded, 16 * N_LOADS)
            eng.tensor_tensor(resets[:, :], dstrow[:, 0, :], dstrow[:, 1, :], ALU.not_equal).then_inc(resets_done, 1)
            eng.wait_ge(resets_done, 1)
            eng.tensor_scalar(resets[:, :], resets[:, :], FAR, None, ALU.mult).then_inc(resets_done, 1)
            eng.wait_ge(prep_mm, 6)
            for h in range(H0):
                eng.tensor_copy(qk[:, h, :], bank[h][:, 0:P]).then_inc(prep_dve, 1)
                eng.tensor_copy(ck[:, h:h + 1], bank[2 + h][:, 0:1]).then_inc(prep_dve, 1)
            eng.tensor_copy(qe[:, :], bank[4][:, 0:ROWS_E]).then_inc(prep_dve, 1)
            eng.tensor_copy(ce[:, :], bank[5][0:ROWS_E, 0:1]).then_inc(prep_dve, 1)
            eng.tensor_scalar(attb[:, :], headmask[:, :], cols[:, 7:8], None, ALU.mult).then_inc(prep_dve, 1)
            eng.tensor_scalar(b1s[:, :], cols[:, 0:2], 0.01, None, ALU.mult).then_inc(prep_dve, 1)
            eng.memset(lastf[:, :], 0.0).then_inc(prep_dve, 1)
            wait_prep(eng)
            a.free_maxima = lambda e, g: None
            a.scores_per_block, a.edge_loads = 1, 48

            def a_step(s):
                g = back(s, 2)
                if active(g):
                    k = parity(g)
                    eng.wait_ge(a.evacuated, total(g, 2))
                    eng.wait_ge(a.edge_in[parity(g)], slot(g, 48))
                    if since(g, 1):
                        eng.wait_ge(a.scored, total(back(g, 1), 1))
                    for h in range(H0):
                        eng.wait_ge(a.projected, part(g, 3, h + 1))
                        eng.scalar_tensor_tensor(out=a.prod[h], in0=bank[2 + h][:, :], scalar=ck[:, h:h + 1], in1=a.xsT[k],
                                                 op0=ALU.add, op1=ALU.mult).then_inc(a.products, 1)
                    eng.wait_ge(a.projected, total(g, 3))
                    eng.scalar_tensor_tensor(out=a.prode, in0=bank[4][0:ROWS_E, :], scalar=ce[:, 0:1], in1=a.ext[k],
                                             op0=ALU.add, op1=ALU.mult).then_inc(a.products, 1)
                g = back(s, 3)
                if active(g):
                    k = parity(g)
                    for h in range(H0):
                        eng.wait_ge(a.spread, part(g, 4, 2 * h + 1))
                        eng.tensor_tensor(a.pv[h], bank[6][:, :], a.xsT[k], ALU.mult).then_inc(a.weighted, 1)
                        eng.wait_ge(a.spread, part(g, 4, 2 * h + 2))
                        eng.wait_ge(a.weighted, part(g, 3, h + 1))
                        if since(g, 2):
                            eng.wait_ge(a.values, total(back(g, 2), LANES))
                        if since(g, 1):
                            eng.wait_ge(a.summed, total(back(g, 1), 3))
                        first = 0.0 if static(g) and g[1] == 0 else a.num[h][1 - k][:, W - 1:W]
                        eng.tensor_tensor_scan(a.num[h][k], bank[7][:, :], a.pv[h], first, ALU.mult, ALU.add).then_inc(a.summed, 1)
                    eng.tensor_tensor(a.pve, a.pd[k][:, 0:W], a.ext[k], ALU.mult).then_inc(a.weighted, 1)
                    eng.wait_ge(a.weighted, total(g, 3))
                    first = 0.0 if static(g) and g[1] == 0 else a.nume[1 - k][:, W - 1:W]
                    eng.tensor_tensor_scan(a.nume[k], a.pd[k][:, W:2 * W], a.pve, first, ALU.mult, ALU.add).then_inc(a.summed, 1)
                g = back(s, 2)
                if active(g):
                    run_maxima(eng, a, bank[5][0:ROWS_E, :], ROWS_E, g)
                g = back(s, 3)
                if active(g):
                    k = parity(g)
                    find_last(eng, a, g)

                    def denominators(j):
                        eng.wait_ge(a.values, part(g, LANES, j + 1))
                        den, rden = a.den[j % 2], a.rden[j % 2]
                        if j >= 2:
                            eng.wait_ge(a.combined, part(g, LANES, j - 1))
                        elif since(g, 1):
                            eng.wait_ge(a.combined, total(back(g, 1), LANES))
                        eng.tensor_scalar(den[:, :], bank[6 + j % 2][:, P:2 * VCOL:VCOL], float(H0), H0 * 1e-16, ALU.mult, ALU.add).then_inc(a.denoms, 1)
                        eng.wait_ge(a.denoms, part(g, 2 * LANES, 2 * j + 1))
                        eng.reciprocal(rden[:, :], den[:, :]).then_inc(a.denoms, 1)

                    def combine(j):
                        eng.wait_ge(a.head0, part(g, LANES, j + 1))
                        o = a.agg[k][:, j * P:(j + 1) * P]
                        eng.wait_ge(a.denoms, part(g, 2 * LANES, 2 * j + 2))
                        eng.scalar_tensor_tensor(out=o, in0=bank[6 + j % 2][:, VCOL:VCOL + P], scalar=a.rden[j % 2][:, 1:2],
                                                 in1=o, op0=ALU.mult, op1=ALU.add).then_inc(a.combined, 1)
                    denominators(0)
                    denominators(1)
                    for j in range(LANES):
                        combine(j)
                        if j + 2 < LANES:
                            denominators(j + 2)
            steps(eng, A_LAGS, a_step)
            wait_scatters(eng, a)

            def b_step(s):
                g = back(s, 1)
                if active(g):
                    k = parity(g)
                    eng.wait_ge(b.skipped, total(g, 1))
                    eng.wait_ge(b.resid, total(g, 2))
                    if since(g, 1):
                        eng.wait_ge(b.ln[0].applied, total(back(g, 1), LANES))
                    eng.tensor_tensor(b.y, bank[0][:, :], b.agg[k], ALU.add).then_inc(b.y_ready, 1)
                    eng.wait_ge(b.y_ready, total(g, 1))
                    norm_vector(eng, b.ln[0], b.y, g)
                g = back(s, 2)
                if active(g):
                    k = parity(g)
                    for h in range(2):
                        eng.wait_ge(b.small_up, part(g, 2, h + 1))
                        if since(g, 1):
                            eng.wait_ge(b.down, total(back(g, 1), 1))
                        eng.scalar_tensor_tensor(out=b.f[h], in0=bank[2 + h][:, :], scalar=cols[:, h:h + 1], in1=b.small[h],
                                                 op0=ALU.add, op1=ALU.max).then_inc(b.act_up, 1)
                    eng.wait_ge(b.down, total(g, 1))
                    if since(g, 1):
                        eng.wait_ge(b.turned2, total(back(g, 1), 1))
                    eng.scalar_tensor_tensor(out=b.y2T, in0=bank[4][:, :], scalar=cols[:, 2:3], in1=b.hT[k],
                                             op0=ALU.add, op1=ALU.add).then_inc(b.y2_ready, 1)
                    eng.wait_ge(b.turned2, total(g, 1))
                    norm_vector(eng, b.ln[1], bank[5], g)
                g = back(s, 3)
                if active(g):
                    k = parity(g)
                    eng.wait_ge(b.y3_ready, total(g, 3))
                    norm_vector(eng, b.ln[2], b.y3[k], g)
                g = back(s, 4)
                if active(g):
                    k = parity(g)
                    eng.wait_ge(b.ln[2].applied, total(g, LANES))
                    norm_vector(eng, b.ln[3], b.x1[k], g)
                    eng.wait_ge(b.normed, total(g, 1))
                    eng.tensor_copy(hnorm[:, bass.ds(at(g, 1), 1), :].rearrange("p a j -> p (a j)"), bank[1][:, 0:LANES]).then_inc(b.hn_saved, 1)
                    if since(g, 2):
                        eng.wait_ge(b.lr_out[parity(back(g, 2))], slot(back(g, 2), 32))
                    for n, dst in enumerate((b.xl[k], b.xr[k])):
                        eng.wait_ge(b.lr, part(g, 2, n + 1))
                        eng.tensor_tensor(lanes(dst), lanes(bank[6 + n][:, :]), rows[:, 3 + n:4 + n, :].to_broadcast([P, LANES, P]), ALU.add).then_inc(b.lr_ready, 1)
            steps(eng, B_LAGS, b_step)
            wait_node_stores(eng)
            eng.memset(c.runmax[:, 2 * W:2 * W + 1], 0.0).then_inc(prep_dve, 1)
            eng.wait_ge(prep_dve, 10)

            def c_free(e, g):
                if since(g, 2):
                    e.wait_ge(c.returned, total(back(g, 2), 2))
            c.free_maxima = c_free
            c.scores_per_block, c.edge_loads = 1, 16

            def c_step(s):
                g = back(s, 2)
                if active(g):
                    k = parity(g)
                    eng.wait_ge(c.turned, total(g, 2))
                    eng.wait_ge(c.evacuated, total(g, 1))
                    if since(g, 1):
                        eng.wait_ge(c.feats, total(back(g, 1), 2))
                    eng.tensor_tensor(c.z, bank[1][:, :], c.xlT[k], ALU.add).then_inc(c.feats, 1)
                    eng.wait_ge(c.feats, part(g, 2, 1))
                    if since(g, 1):
                        eng.wait_ge(c.scored, total(back(g, 1), 1))
                    eng.scalar_tensor_tensor(out=c.leaky, in0=c.z, scalar=0.2, in1=c.z, op0=ALU.mult, op1=ALU.max).then_inc(c.feats, 1)
                g = back(s, 3)
                if active(g):
                    k = parity(g)
                    eng.wait_ge(c.weights, total(g, 1))
                    eng.tensor_tensor(c.pv, c.pd[k][:, 0:W], c.xlT[k], ALU.mult).then_inc(c.weighted, 1)
                    if since(g, 2):
                        eng.wait_ge(c.returned, total(back(g, 2), 2))
                    if since(g, 1):
                        eng.wait_ge(c.summed, total(back(g, 1), 2))
                    start = static(g) and g[1] == 0
                    eng.tensor_tensor_scan(c.den[k], c.pd[k][:, W:2 * W], c.pd[k][:, 0:W],
                                           0.0 if start else c.den[1 - k][:, W - 1:W], ALU.mult, ALU.add).then_inc(c.summed, 1)
                    eng.wait_ge(c.weighted, total(g, 1))
                    eng.tensor_tensor_scan(c.num[k], c.pd[k][:, W:2 * W], c.pv,
                                           0.0 if start else c.num[1 - k][:, W - 1:W], ALU.mult, ALU.add).then_inc(c.summed, 1)
                g = back(s, 2)
                if active(g):
                    run_maxima(eng, c, bank[2][:, :], P, g)
                g = back(s, 3)
                if active(g):
                    k = parity(g)
                    find_last(eng, c, g)
                    eng.wait_ge(c.returned, total(g, 2))
                    eng.tensor_copy(c.row[k].rearrange("p (j f) -> p j f", j=LANES)[:, :, P:GROW],
                                    bank[4][:, 0:LANES * 2 * H1].rearrange("p (j f) -> p j f", j=LANES)).then_inc(c.packed, 1)
            steps(eng, A_LAGS, c_step)
            wait_scatters(eng, c)

            eng.wait_ge(hnorm_ready, 1)

            def gcols(ap, first):
                return ap.rearrange("p (j f) -> p j f", j=LANES)[:, :, P + first:P + first + H1]

            def jh(ap):
                return ap.rearrange("p (j h) -> p j h", j=LANES)

            def d_step(s):
                g = back(s, 1)
                if active(g):
                    k = parity(g)
                    eng.wait_ge(d.node_in[parity(g)], slot(g, 64))
                    eng.wait_ge(d.z_ready, total(g, 1))
                    if since(g, 1):
                        eng.wait_ge(d.self_ready, total(back(g, 1), 1))
                    eng.scalar_tensor_tensor(out=d.lk, in0=d.z, scalar=0.2, in1=d.z, op0=ALU.mult, op1=ALU.max).then_inc(d.lk_ready, 1)
                    eng.wait_ge(d.la_ready, total(g, 1))
                    if since(g, 1):
                        eng.wait_ge(d.diffs, total(back(g, 1), 2))
                    eng.tensor_reduce(d.self_s[:, :], heads(d.lk), AX.X, ALU.add).then_inc(d.self_ready, 1)
                    eng.wait_ge(d.self_ready, total(g, 1))
                    eng.tensor_tensor(jh(d.top[:, :]), gcols(d.g[k], H1), jh(d.self_s[:, :]), ALU.max).then_inc(d.top_ready, 1)
                    eng.wait_ge(d.top_ready, total(g, 1))
                    if since(g, 1):
                        eng.wait_ge(d.exps, total(back(g, 1), 1))
                    eng.tensor_tensor(jh(d.diff[:, 0, :]), gcols(d.g[k], H1), jh(d.top[:, :]), ALU.subtract).then_inc(d.diffs, 1)
                    eng.tensor_tensor(d.diff[:, 1, :], d.self_s[:, :], d.top[:, :], ALU.subtract).then_inc(d.diffs, 1)
                g = back(s, 2)
                if active(g):
                    k = parity(g)
                    eng.wait_ge(d.exps, total(g, 1))
                    if since(g, 1):
                        eng.wait_ge(d.shares, total(back(g, 1), 4))
                    eng.tensor_tensor(jh(d.dn[:, :]), gcols(d.g[k], 0), jh(d.ex[k][:, 0, :]), ALU.mult).then_inc(d.shares, 1)
                    eng.wait_ge(d.shares, part(g, 4, 1))
                    eng.tensor_tensor(d.dn[:, :], d.dn[:, :], d.ex[k][:, 1, :], ALU.add).then_inc(d.shares, 1)
                    eng.wait_ge(d.shares, part(g, 4, 2))
                    eng.reciprocal(d.dn[:, :], d.dn[:, :]).then_inc(d.shares, 1)
                    eng.wait_ge(d.shares, part(g, 4, 3))
                    eng.tensor_tensor(d.ex[k][:, :, :], d.ex[k][:, :, :], d.dn[:, :].unsqueeze(1).to_broadcast([P, 2, LANES * H1]), ALU.mult).then_inc(d.shares, 1)
                    eng.wait_ge(d.shares, total(g, 4))
                    if since(g, 1):
                        eng.wait_ge(d.sq_ready, total(back(g, 1), LANES))
                    if since(g, 1):
                        eng.wait_ge(d.y_ready, total(back(g, 1), LANES))
                    eng.tensor_tensor(heads(d.o2), heads(d.xl[k]), wide(d.ex[k][:, 1, :]), ALU.mult).then_inc(d.part_s, 1)
                    eng.wait_ge(d.part_s, total(g, 1))
                    eng.wait_ge(d.part_e, total(g, 1))
                    eng.tensor_tensor(d.o2, d.o2, d.o, ALU.add).then_inc(d.sum_es, 1)
                    eng.wait_ge(d.nrm_ready, total(g, 1))
                    if since(g, 1):
                        eng.wait_ge(d.y_ready, total(back(g, 1), LANES))
                    eng.tensor_scalar(d.fac[:, :], d.nrm[:, :], 1e-12, None, ALU.max).then_inc(d.fac_ready, 1)
                    eng.wait_ge(d.fac_ready, part(g, 4, 1))
                    eng.reciprocal(d.fac[:, :], d.fac[:, :]).then_inc(d.fac_ready, 1)
                    eng.wait_ge(d.fac_ready, part(g, 4, 2))
                    eng.tensor_tensor(d.fac[:, :], d.fac[:, :], hnorm[:, bass.ds(at(g, 1), 1), :].rearrange("p a j -> p (a j)"), ALU.mult).then_inc(d.fac_ready, 1)
                    eng.wait_ge(d.fac_ready, part(g, 4, 3))
                    eng.tensor_scalar(d.fac[:, :], d.fac[:, :], scalec[:, 0:1], None, ALU.mult).then_inc(d.fac_ready, 1)
                    eng.wait_ge(d.fac_ready, total(g, 4))
                    if since(g, 2):
                        eng.wait_ge(d.ln.applied, total(back(g, 2), LANES))
                    eng.wait_ge(d.doubled, total(g, 1))
                    for j in range(LANES):
                        q = slice(j * P, (j + 1) * P)
                        eng.scalar_tensor_tensor(out=d.y[k][:, q], in0=d.o2[:, q], scalar=d.fac[:, j:j + 1], in1=d.x1[k][:, q],
                                                 op0=ALU.mult, op1=ALU.add).then_inc(d.y_ready, 1)
                g = back(s, 3)
                if active(g):
                    k = parity(g)
                    eng.wait_ge(d.y_ready, total(g, LANES))
                    norm_vector(eng, d.ln, d.y[k], g)
            steps(eng, D_LAGS, d_step)

        @block.scalar
        def _(eng):
            wait_prep(eng)
            score_scale = float(P) ** -0.5

            def a_step(s):
                g = back(s, 1)
                if active(g):
                    k = parity(g)
                    if since(g, 2):
                        eng.wait_ge(a.weighted, total(back(g, 2), 3))
                    if since(g, 2):
                        eng.wait_ge(a.projected, total(back(g, 2), 3))
                    eng.wait_ge(a.turned, part(g, 2, 1))
                    eng.activation(a.xsT[k], bank[0][:, :], ACT.Copy).then_inc(a.evacuated, 1)
                    eng.wait_ge(a.turned, total(g, 2))
                    eng.activation(a.xdT[k], bank[1][:, :], ACT.Copy).then_inc(a.evacuated, 1)
                g = back(s, 2)
                if active(g):
                    k = parity(g)
                    eng.wait_ge(a.shifts, total(g, 3))
                    if since(g, 2):
                        eng.wait_ge(a.summed, total(back(g, 2), 3))
                    if since(g, 2):
                        eng.wait_ge(a.spread, total(back(g, 2), 4))
                    eng.activation(a.pd[k], a.shift, ACT.Exp, scale=score_scale).then_inc(a.weights, 1)
                g = back(s, 3)
                if active(g):
                    k = parity(g)
                    if since(g, 2):
                        eng.wait_ge(a.scattered[parity(back(g, 2))], slot(back(g, 2), 16 * LANES))
                    for j in range(LANES):
                        eng.wait_ge(a.denoms, part(g, 2 * LANES, 2 * j + 2))
                        eng.activation(a.agg[k][:, j * P:(j + 1) * P], bank[6 + j % 2][:, 0:P], ACT.Copy,
                                       scale=a.rden[j % 2][:, 0:1]).then_inc(a.head0, 1)
            steps(eng, A_LAGS, a_step)
            wait_scatters(eng, a)

            def b_step(s):
                g = back(s, 1)
                if active(g):
                    k = parity(g)
                    if since(g, 1):
                        eng.wait_ge(b.turned1, total(back(g, 1), 1))
                    norm_scalar(eng, b.ln[0], b.y, b.z, g)
                    eng.wait_ge(b.turned1, total(g, 1))
                    if since(g, 2):
                        eng.wait_ge(b.up, total(back(g, 2), 2))
                    if since(g, 2):
                        eng.wait_ge(b.y2_ready, total(back(g, 2), 1))
                    eng.activation(b.hT[k], bank[1][:, :], ACT.Identity, bias=cols[:, 4:5], scale=cols[:, 3:4]).then_inc(b.h_ready, 1)
                g = back(s, 2)
                if active(g):
                    k = parity(g)
                    for h in range(2):
                        eng.wait_ge(b.up, part(g, 2, h + 1))
                        if since(g, 1):
                            eng.wait_ge(b.act_up, total(back(g, 1), 2))
                        eng.activation(b.small[h], bank[2 + h][:, :], ACT.Identity, bias=b1s[:, h:h + 1], scale=0.01).then_inc(b.small_up, 1)
                    if since(g, 1):
                        eng.wait_ge(b.y3_ready, total(back(g, 1), 3))
                    norm_scalar(eng, b.ln[1], bank[5], b.z2, g)
                g = back(s, 3)
                if active(g):
                    k = parity(g)
                    if since(g, 2):
                        eng.wait_ge(b.x1_out[parity(back(g, 2))], slot(back(g, 2), 16))
                    if since(g, 2):
                        eng.wait_ge(b.ln[3].applied, total(back(g, 2), LANES))
                    norm_scalar(eng, b.ln[2], b.y3[k], b.x1[k], g)
                g = back(s, 4)
                if active(g):
                    k = parity(g)
                    if since(g, 1):
                        eng.wait_ge(b.turned4, total(back(g, 1), 1))
                    norm_scalar(eng, b.ln[3], b.x1[k], b.z4, g)
                    eng.wait_ge(b.turned4, total(g, 1))
                    if since(g, 1):
                        eng.wait_ge(b.lr, total(back(g, 1), 2))
                    eng.activation(b.h1T, bank[1][:, :], ACT.Relu, bias=cols[:, 6:7], scale=cols[:, 5:6]).then_inc(b.h1_ready, 1)
                    eng.wait_ge(b.h1_ready, total(g, 1))
                    if since(g, 1):
                        eng.wait_ge(b.normed, total(back(g, 1), 1))
                    eng.activation(b.sq, b.h1T, ACT.Square).then_inc(b.squared, 1)
            steps(eng, B_LAGS, b_step)
            wait_node_stores(eng)
            eng.wait_ge(b.hn_saved, BLOCKS)
            eng.activation(hnorm[:, :, :], hnorm[:, :, :], ACT.Sqrt).then_inc(hnorm_ready, 1)

            def c_step(s):
                g = back(s, 1)
                if active(g):
                    k = parity(g)
                    if since(g, 2):
                        eng.wait_ge(c.weighted, total(back(g, 2), 1))
                    eng.wait_ge(c.turned, part(g, 2, 1))
                    eng.activation(c.xlT[k], bank[0][:, :], ACT.Copy).then_inc(c.evacuated, 1)
                g = back(s, 2)
                if active(g):
                    k = parity(g)
                    eng.wait_ge(c.shifts, total(g, 3))
                    if since(g, 2):
                        eng.wait_ge(c.summed, total(back(g, 2), 2))
                    if since(g, 2):
                        eng.wait_ge(c.weighted, total(back(g, 2), 1))
                    eng.activation(c.pd[k], c.shift, ACT.Exp).then_inc(c.weights, 1)
                g = back(s, 3)
                if active(g):
                    k = parity(g)
                    eng.wait_ge(c.returned, part(g, 2, 1))
                    if since(g, 2):
                        eng.wait_ge(c.scattered[parity(back(g, 2))], slot(back(g, 2), 16 * LANES))
                    eng.activation(c.row[k].rearrange("p (j f) -> p j f", j=LANES)[:, :, 0:P], lanes(bank[3][:, :]), ACT.Copy).then_inc(c.packed, 1)
            steps(eng, A_LAGS, c_step)
            wait_scatters(eng, c)

            def d_step(s):
                g = back(s, 1)
                if active(g):
                    k = parity(g)
                    eng.wait_ge(d.diffs, total(g, 2))
                    if since(g, 2):
                        eng.wait_ge(d.part_e, total(back(g, 2), 1))
                    if since(g, 2):
                        eng.wait_ge(d.part_s, total(back(g, 2), 1))
                    eng.activation(d.ex[k][:, :, :], d.diff[:, :, :], ACT.Exp).then_inc(d.exps, 1)
                g = back(s, 2)
                if active(g):
                    eng.wait_ge(d.o_ready, total(g, 1))
                    for j in range(LANES):
                        q = slice(j * P, (j + 1) * P)
                        if j == 0:
                            if since(g, 1):
                                eng.wait_ge(d.nrm_ready, total(back(g, 1), 1))
                        eng.activation(d.sq[:, q], d.o2[:, q], ACT.Square, accum_out=d.ss[:, j:j + 1]).then_inc(d.sq_ready, 1)
                    eng.wait_ge(d.sq_ready, total(g, LANES))
                    if since(g, 1):
                        eng.wait_ge(d.fac_ready, total(back(g, 1), 4))
                    eng.activation(d.nrm[:, :], d.ss[:, :], ACT.Sqrt).then_inc(d.nrm_ready, 1)
                g = back(s, 3)
                if active(g):
                    k = parity(g)
                    if since(g, 2):
                        eng.wait_ge(d.out_done[parity(back(g, 2))], slot(back(g, 2), 16))
                    norm_scalar(eng, d.ln, d.y[k], d.res[k], g)
            steps(eng, D_LAGS, d_step)

        @block.tensor
        def _(eng):
            eng.wait_ge(loaded, 16 * N_LOADS)
            for h in range(H0):
                eng.matmul(bank[h][:, 0:P], wq[:, h, :], wk[:, h, :], start=True, stop=True).then_inc(prep_mm, 1)
                eng.matmul(bank[2 + h][:, 0:1], wk[:, h, :], bq[:, h:h + 1], start=True, stop=True).then_inc(prep_mm, 1)
            for h in range(H0):
                mm = eng.matmul(bank[4][:, 0:ROWS_E], wq[:, h, :], wexb[:, h, :], start=h == 0, stop=h == H0 - 1)
            mm.then_inc(prep_mm, 1)
            for h in range(H0):
                mm = eng.matmul(bank[5][0:ROWS_E, 0:1], wexb[:, h, :], bq[:, h:h + 1], start=h == 0, stop=h == H0 - 1)
            mm.then_inc(prep_mm, 1)
            wait_prep(eng)

            def turn(dst, src, done):
                for j in range(LANES):
                    mm = eng.transpose(dst[:, j * P:(j + 1) * P], src[:, j * P:(j + 1) * P], ident[:, :])
                mm.then_inc(done, 1)

            def a_step(s):
                g = back(s, 2)
                if active(g):
                    k = parity(g)
                    eng.wait_ge(a.evacuated, total(g, 2))
                    if since(g, 1):
                        eng.wait_ge(a.products, total(back(g, 1), 3))
                    for h in range(H0):
                        eng.matmul(bank[2 + h][:, :], qk[:, h, :], a.xdT[k], start=True, stop=True).then_inc(a.projected, 1)
                    eng.matmul(bank[4][0:ROWS_E, :], qe[:, :], a.xdT[k], start=True, stop=True).then_inc(a.projected, 1)
                g = back(s, 3)
                if active(g):
                    k = parity(g)
                    eng.wait_ge(a.weights, total(g, 1))
                    if since(g, 1):
                        eng.wait_ge(a.combined, total(back(g, 1), LANES))
                    for h in range(H0):
                        if h:
                            eng.wait_ge(a.weighted, part(g, 3, h))
                        eng.matmul(bank[6][:, :], spread_w[:, h, :], a.pd[k][:, 0:W], start=True, stop=True).then_inc(a.spread, 1)
                        if h:
                            eng.wait_ge(a.summed, part(g, 3, h))
                        eng.matmul(bank[7][:, :], spread_w[:, h, :], a.pd[k][:, W:2 * W], start=True, stop=True).then_inc(a.spread, 1)
                g = back(s, 1)
                if active(g):
                    k = parity(g)
                    eng.wait_ge(a.gathered[parity(g)], slot(g, 2 * 16 * LANES))
                    if since(g, 1):
                        eng.wait_ge(a.evacuated, total(back(g, 1), 2))
                    turn(bank[0], a.xs[k], a.turned)
                    turn(bank[1], a.xd[k], a.turned)
                g = back(s, 2)
                if active(g):
                    k = parity(g)
                    eng.wait_ge(a.products, total(g, 3))
                    if since(g, 1):
                        eng.wait_ge(a.shifts, total(back(g, 1), 3))
                    eng.matmul(bank[5][0:ROWS_E, :], sumx[:, 0, :], a.prod[0], start=True, stop=False)
                    eng.matmul(bank[5][0:ROWS_E, :], sumx[:, 1, :], a.prod[1], start=False, stop=False)
                    eng.matmul(bank[5][0:ROWS_E, :], sume[:, :], a.prode, start=False, stop=True).then_inc(a.scored, 1)
                g = back(s, 3)
                if active(g):
                    k = parity(g)
                    eng.wait_ge(a.summed, total(g, 3))
                    for j in range(LANES):
                        q = slice(j * P, (j + 1) * P)
                        o = bank[6 + j % 2]
                        if j >= 2:
                            eng.wait_ge(a.combined, part(g, LANES, j - 1))
                        eng.matmul(o[:, 0:H0 * VCOL], a.nume[k][:, q], wve[:, :, :].rearrange("p h c -> p (h c)"), start=True, stop=False)
                        eng.matmul(o[:, 0:P], a.num[0][k][:, q], wv[:, 0, :], start=False, stop=False)
                        eng.matmul(o[:, VCOL:VCOL + P], a.num[1][k][:, q], wv[:, 1, :], start=False, stop=True).then_inc(a.values, 1)
            steps(eng, A_LAGS, a_step)
            wait_scatters(eng, a)

            def b_step(s):
                g = back(s, 1)
                if active(g):
                    k = parity(g)
                    eng.wait_ge(b.node_in[parity(g)], slot(g, 48))
                    if since(g, 1):
                        eng.wait_ge(b.y_ready, total(back(g, 1), 1))
                    for j in range(LANES):
                        q = slice(j * P, (j + 1) * P)
                        mm = eng.matmul(bank[0][:, q], b.xT[k][:, q], wskip[:, :], start=True, stop=True)
                    mm.then_inc(b.skipped, 1)
                    eng.wait_ge(b.ln[0].applied, total(g, LANES))
                    if since(g, 4):
                        eng.wait_ge(b.hn_saved, total(back(g, 4), 1))
                    turn(bank[1], b.z, b.turned1)
                g = back(s, 2)
                if active(g):
                    k = parity(g)
                    eng.wait_ge(b.h_ready, total(g, 1))
                    if since(g, 1):
                        eng.wait_ge(b.act_up, total(back(g, 1), 2))
                    for h in range(2):
                        eng.matmul(bank[2 + h][:, :], w1[:, h, :], b.hT[k], start=True, stop=True).then_inc(b.up, 1)
                    eng.wait_ge(b.act_up, total(g, 2))
                    if since(g, 1):
                        eng.wait_ge(b.y2_ready, total(back(g, 1), 1))
                    eng.matmul(bank[4][:, :], w2[:, 0, :], b.f[0], start=True, stop=False)
                    eng.matmul(bank[4][:, :], w2[:, 1, :], b.f[1], start=False, stop=True).then_inc(b.down, 1)
                    eng.wait_ge(b.y2_ready, total(g, 1))
                    if since(g, 1):
                        eng.wait_ge(b.ln[1].applied, total(back(g, 1), LANES))
                    turn(bank[5], b.y2T, b.turned2)
                g = back(s, 4)
                if active(g):
                    k = parity(g)
                    eng.wait_ge(b.ln[3].applied, total(g, LANES))
                    eng.wait_ge(b.h_ready, total(within(back(g, -3)), 1))
                    turn(bank[1], b.z4, b.turned4)
                    eng.wait_ge(b.h1_ready, total(g, 1))
                    if since(g, 1):
                        eng.wait_ge(b.lr_ready, total(back(g, 1), 2))
                    for n in range(2):
                        for j in range(LANES):
                            q = slice(j * P, (j + 1) * P)
                            mm = eng.matmul(bank[6 + n][:, q], b.h1T[:, q], wlr[:, n, :], start=True, stop=True)
                        mm.then_inc(b.lr, 1)
                    eng.wait_ge(b.squared, total(g, 1))
                    for j in range(LANES):
                        mm = eng.matmul(bank[1][:, j:j + 1], b.sq[:, j * P:(j + 1) * P], ones[:, 0:1], start=True, stop=True)
                    mm.then_inc(b.normed, 1)
            steps(eng, B_LAGS, b_step)
            wait_node_stores(eng)

            def c_step(s):
                g = back(s, 1)
                if active(g):
                    k = parity(g)
                    eng.wait_ge(c.gathered[parity(g)], slot(g, 2 * 16 * LANES))
                    if since(g, 1):
                        eng.wait_ge(c.evacuated, total(back(g, 1), 1))
                    turn(bank[0], c.xl[k], c.turned)
                    if since(g, 1):
                        eng.wait_ge(c.feats, total(back(g, 1), 2))
                    turn(bank[1], c.xr[k], c.turned)
                g = back(s, 2)
                if active(g):
                    eng.wait_ge(c.feats, total(g, 2))
                    if since(g, 1):
                        eng.wait_ge(c.shifts, total(back(g, 1), 3))
                    eng.matmul(bank[2][:, :], attb[:, :], c.leaky, start=True, stop=True).then_inc(c.scored, 1)
                g = back(s, 3)
                if active(g):
                    k = parity(g)
                    eng.wait_ge(c.summed, total(g, 2))
                    if since(g, 1):
                        eng.wait_ge(c.packed, total(back(g, 1), 2))
                    turn(bank[3], c.num[k], c.returned)
                    for j in range(LANES):
                        q = slice(j * P, (j + 1) * P)
                        eng.matmul(bank[4][:, j * 2 * H1:j * 2 * H1 + H1], c.den[k][:, q], headpick[:, :], start=True, stop=True)
                        o = k * W + 1 + j * P
                        mm = eng.matmul(bank[4][:, j * 2 * H1 + H1:(j + 1) * 2 * H1], c.runmax[:, o:o + P], headpick[:, :], start=True, stop=True)
                    mm.then_inc(c.returned, 1)
            steps(eng, A_LAGS, c_step)


A_LAGS, B_LAGS, D_LAGS = 4, 4, 3


def kernel(**inputs):
    import numpy as _np
    import concourse.bacc as _bacc
    from concourse import mybir as _mybir
    from concourse.bass_utils import run_bass_kernel_spmd as _run

    v = {k: _np.asarray(a) for k, a in inputs.items()}
    l0 = {k[7:]: a for k, a in v.items() if k.startswith("L0_gnn_")}
    l1 = {k[7:]: a for k, a in v.items() if k.startswith("L1_gnn_")}
    f32 = _np.float32
    pad = NP - N_NODES
    x = _np.concatenate([v["x"], _np.zeros((pad, P), f32)])
    xT = x.reshape(BLOCKS, P, LANES, P).transpose(3, 0, 2, 1).reshape(P, NP)
    src = _np.concatenate([v["src"], _np.zeros(pad, _np.int32)])
    dst = _np.concatenate([v["dst"], _np.full(pad, N_NODES, _np.int32)])
    none = _np.full(1, NP, _np.int32)
    nxt = _np.concatenate([dst[1:], none])
    prev = _np.concatenate([none, dst[:-1]])
    idx = _np.stack([src, dst, nxt]).reshape(3, BLOCKS, LANES, P).transpose(1, 3, 0, 2)
    dstrow = _np.stack([dst.reshape(BLOCKS, W), prev.reshape(BLOCKS, W)], axis=1)
    eaT = _np.concatenate([v["edge_attr_32"], _np.zeros((pad, EDIM), f32)]).T

    head_of = _np.array([r // EDIM if r < DEN0 else r - DEN0 for r in range(ROWS_E)])
    own = (head_of[:, None] == _np.arange(H0)[None, :]).astype(f32)
    sumx = _np.broadcast_to(own.T[None], (P, H0, ROWS_E))
    sume = (head_of[:, None] == head_of[None, :]).astype(f32)
    spread_w = _np.zeros((ROWS_E, H0, P), f32)
    wexb = _np.zeros((P, H0, ROWS_E), f32)
    wve = _np.zeros((ROWS_E, H0, VCOL), f32)
    for h in range(H0):
        c = slice(h * P, (h + 1) * P)
        e = slice(h * EDIM, (h + 1) * EDIM)
        spread_w[DEN0 + h, h, :] = 1
        wexb[:, h, e] = l0["We"][c]
        wexb[:, h, DEN0 + h] = l0["bk"][c]
        wve[e, h, 0:P] = l0["We"][c].T
        wve[DEN0 + h, h, 0:P] = l0["bv"][c]
        wve[DEN0 + h, h, P] = 1
    att = l1["att"].reshape(P)
    lane = _np.arange(P)
    arrays = {
        "x": x, "xT": xT, "idx": idx, "dstrow": dstrow, "eaT": eaT,
        "ident": _np.eye(P, dtype=f32),
        "headmask": (lane[:, None] // C1 == lane[None, :] // C1).astype(f32),
        "headpick": (lane[:, None] == C1 * _np.arange(H1)[None, :]).astype(f32),
        "sumx": sumx, "sume": sume, "spread_w": spread_w,
        "Wq": l0["Wq"], "Wk": l0["Wk"], "wexb": wexb, "bq": l0["bq"].reshape(H0, P).T,
        "WvT": l0["Wv"].T, "wve": wve, "WskipT": l0["Wskip"].T, "W1T": l0["W1"].T, "W2T": l0["W2"].T,
        "W_l": l1["W_l"], "W_r": l1["W_r"],
        "cols": _np.stack([l0["b1"][:P], l0["b1"][P:], l0["b2"], l0["ln1_g"], l0["ln1_b"],
                           l1["gamma"], l1["beta"], att], axis=1),
        "rows": _np.stack([l0["bskip"], l0["ln2_g"], l0["ln2_b"], l1["b_l"], l1["b_r"], att, l1["bias"]]),
        "scale": l1["scale"].reshape(1),
    }
    arrays = {k: _np.ascontiguousarray(a) for k, a in arrays.items()}
    nc = _bacc.Bacc("TRN2", target_bir_lowering=False, num_devices=1)
    t = {k: nc.dram_tensor("in_" + k, a.shape, _mybir.dt.from_np(a.dtype), kind="ExternalInput").ap() for k, a in arrays.items()}
    out = nc.dram_tensor("out", (NP, P), F32, kind="ExternalOutput").ap()
    build(nc, t, out)
    r = _run(nc, [{"in_" + k: a for k, a in arrays.items()}], core_ids=[0])
    return r.results[0]["out"][:N_NODES]
```

```python
from contextlib import ExitStack

import concourse.bass as bass
from concourse import mybir

F32 = mybir.dt.float32
I32 = mybir.dt.int32
U32 = mybir.dt.uint32
ALU = mybir.AluOpType
ACT = mybir.ActivationFunctionType
AX = mybir.AxisListType

P = 128
LANES = 4
W = P * LANES
N_NODES = 50000
BLOCKS = -(-N_NODES // W)
NP = BLOCKS * W
H0, H1 = 2, 4
C1 = P // H1
EDIM = 32
ROWS_E = H0 * EDIM + H0
DEN0 = H0 * EDIM
VCOL = P + 1
GROW = P + 2 * H1
SKIP = 1048576
FAR = -1e30
FILL = 14
EPS = 1e-5
UNROLL = 8
REACH = 2


class Phase:
    pass


def back(blk, lag):
    return blk[0], blk[1] - lag


def parity(blk):
    return blk[1] % 2


def at(blk, size):
    return blk[0] * (2 * size) + blk[1] * size


def static(blk):
    return isinstance(blk[0], int)


def total(blk, per_block):
    return at(blk, per_block) + per_block


def part(blk, per_block, done):
    return at(blk, per_block) + done


def slot(blk, per_block):
    return blk[0] * per_block + (blk[1] // 2 + 1) * per_block


def since(blk, lag):
    return not static(blk) or blk[1] >= lag


def steps(eng, lags, body, unroll=UNROLL):
    head = (lags + REACH + 1) // 2
    head += (BLOCKS // 2 - head) % (unroll // 2)
    for s in range(2 * head):
        body((0, s))
    with eng.Fori(head, BLOCKS // 2 - unroll // 2 + 1, unroll // 2) as i:
        for u in range(unroll):
            body((i, u))
    for s in range(BLOCKS, BLOCKS + lags):
        body((0, s))


def active(blk):
    return not static(blk) or 0 <= blk[1] < BLOCKS


def within(blk):
    return (0, min(blk[1], BLOCKS - 1)) if static(blk) else blk


def build(nc, t, out):
    ctx = ExitStack()
    with ctx:
        def sb(name, shape, dt=F32):
            return ctx.enter_context(nc.sbuf_tensor(name, shape, dt))

        def sem(name):
            return ctx.enter_context(nc.semaphore(name))

        def sem2(name):
            return [sem(f"{name}_{k}") for k in range(2)]

        reset_d = nc.dram_tensor("reset_d", (BLOCKS, W), F32, kind="Internal").ap()
        agg_d = nc.dram_tensor("agg_d", (NP, P), F32, kind="Internal").ap()
        x1_d = nc.dram_tensor("x1_d", (NP, P), F32, kind="Internal").ap()
        xl_d = nc.dram_tensor("xl_d", (NP, P), F32, kind="Internal").ap()
        xr_d = nc.dram_tensor("xr_d", (NP, P), F32, kind="Internal").ap()
        gat_d = nc.dram_tensor("gat_d", (NP, GROW), F32, kind="Internal").ap()

        ident = sb("ident", [P, P])
        wq = sb("wq", [P, H0, P])
        wk = sb("wk", [P, H0, P])
        wexb = sb("wexb", [P, H0, ROWS_E])
        bq = sb("bq", [P, H0])
        qk = sb("qk", [P, H0, P])
        qe = sb("qe", [P, ROWS_E])
        ck = sb("ck", [P, H0])
        ce = sb("ce", [ROWS_E, 1])
        sumx = sb("sumx", [P, H0, ROWS_E])
        sume = sb("sume", [ROWS_E, ROWS_E])
        spread_w = sb("spread_w", [ROWS_E, H0, P])
        wv = sb("wv", [P, H0, P])
        wve = sb("wve", [ROWS_E, H0, VCOL])
        wskip = sb("wskip", [P, P])
        w1 = sb("w1", [P, 2, P])
        w2 = sb("w2", [P, 2, P])
        wlr = sb("wlr", [P, 2, P])
        cols = sb("cols", [P, 8])
        b1s = sb("b1s", [P, 2])
        rows = sb("rows", [P, 7, P])
        attb = sb("attb", [P, P])
        headmask = sb("headmask", [P, P])
        headpick = sb("headpick", [P, H1])
        ones = sb("ones", [P, 1])
        epsc = sb("epsc", [P, 1])
        scalec = sb("scalec", [P, 1])
        hnorm = sb("hnorm", [P, BLOCKS, LANES])
        selfs = sb("selfs", [P, BLOCKS, LANES * H1])
        fill = sb("fill", [P, LANES, GROW])
        zeros = sb("zeros", [P, FILL, P])
        dstrow = sb("dstrow", [BLOCKS, 2, W], I32)
        resets = sb("resets", [BLOCKS, W])

        ARENA = 46
        arena = sb("arena", [P, ARENA, W + 4])
        taken = [0]

        def phase_tiles():
            taken[0] = 0

        def tile(parts=P, width=W):
            k = taken[0]
            n = -(-width // (W + 4))
            taken[0] += n
            assert taken[0] <= ARENA, taken
            return arena[0:parts, k:k + n, :].rearrange("p a w -> p (a w)")[:, 0:width]

        def tile2(parts=P, width=W):
            return [tile(parts, width) for _ in range(2)]

        def lanes(ap):
            return ap.rearrange("p (j f) -> p j f", j=LANES)

        bank = [ctx.enter_context(nc.psum_tensor(f"bank{k}", [P, W], F32)) for k in range(8)]

        y2_bank = [bank[0], bank[5]]
        value_bank = [bank[6], bank[7], bank[0], bank[1]]
        idx = [sb(f"idx{k}", [P, 2, LANES], I32) for k in range(2)]
        ends = [sb(f"ends{k}", [P, 2, LANES], I32) for k in range(2)]
        lastf = sb("lastf", [P, LANES])
        last = [sb(f"last{k}", [P, LANES], I32) for k in range(2)]

        loaded = sem("weights_loaded")
        memset_done = sem("memset_done")
        prep_mm = sem("prep_products")
        prep_dve = sem("prep_vector")
        resets_done = sem("resets_computed")
        reset_stored = sem("resets_stored")
        hnorm_ready = sem("hnorm_ready")

        a = Phase()
        phase_tiles()
        a.xs, a.xd = tile2(), tile2()
        a.xsT, a.xdT = tile2(), tile2()
        a.ext, a.reset = tile2(ROWS_E), tile2(ROWS_E)
        a.prod = [tile(), tile()]
        a.prode = tile(ROWS_E)
        a.runmax = tile(ROWS_E, 2 * W + 1)
        a.shift = tile(ROWS_E, 2 * W)
        a.pd = [tile(ROWS_E, 2 * W), tile(ROWS_E, 2 * W)]
        a.pv = [tile(), tile()]
        a.pve = tile(ROWS_E)
        a.num = [tile2(), tile2()]
        a.nume = tile2(ROWS_E)
        a.agg = tile2()
        a.den = sb("a_den", [P, LANES, H0])
        a.rden = sb("a_rden", [P, LANES, H0])
        a.filled = sem("a_filled")
        a.turned = sem("a_turned")
        a.evacuated = sem("a_evacuated")
        a.projected = sem("a_projected")
        a.products = sem("a_products")
        a.scored = sem("a_scored")
        a.maxima = sem("a_maxima")
        a.shifts = sem("a_shifts")
        a.weights = sem("a_weights")
        a.spread = sem("a_spread")
        a.weighted = sem("a_weighted")
        a.summed = sem("a_summed")
        a.values = sem("a_values")
        a.denoms = sem("a_denoms")
        a.head0 = sem("a_head0")
        a.combined = sem("a_combined")
        a.carried = sem("a_carried")
        a.lastrow = sem("a_lastrow")
        a.go = sem("a_go")
        a.idx_in = sem2("a_idx_in")
        a.ends_in = sem2("a_ends_in")
        a.edge_in = sem2("a_edge_in")
        a.gathered = sem2("a_gathered")
        a.scattered = sem2("a_scattered")

        c = Phase()
        phase_tiles()
        c.xl, c.xr = tile2(), tile2()
        c.xlT = tile2()
        c.reset = tile2()
        c.z, c.leaky = tile(), tile()
        c.runmax = tile(P, 2 * W + 1)
        c.shift = tile(P, 2 * W)
        c.pd = [tile(P, 2 * W), tile(P, 2 * W)]
        c.pv = tile()
        c.num, c.den = tile2(), tile2()
        c.own_l, c.own_r = tile2(), tile2()
        c.own_z = tile()
        c.self_scored = sem("c_self_scored")
        c.own_in = sem2("c_own_in")
        c.row = [tile(P, LANES * GROW), tile(P, LANES * GROW)]
        c.filled = sem("c_filled")
        c.turned = sem("c_turned")
        c.evacuated = sem("c_evacuated")
        c.feats = sem("c_feats")
        c.scored = sem("c_scored")
        c.maxima = sem("c_maxima")
        c.shifts = sem("c_shifts")
        c.weights = sem("c_weights")
        c.weighted = sem("c_weighted")
        c.summed = sem("c_summed")
        c.returned = sem("c_returned")
        c.packed = sem("c_packed")
        c.carried = sem("c_carried")
        c.lastrow = sem("c_lastrow")
        c.go = sem("c_go")
        c.idx_in = sem2("c_idx_in")
        c.ends_in = sem2("c_ends_in")
        c.edge_in = sem2("c_edge_in")
        c.gathered = sem2("c_gathered")
        c.scattered = sem2("c_scattered")

        def stats_tiles(name):
            q = Phase()
            q.stats = sb(name + "_stats", [P, LANES, 6])
            q.mv = sb(name + "_mv", [P, LANES, 2])
            q.sd = sb(name + "_sd", [P, LANES])
            q.rstd = sb(name + "_rstd", [P, LANES])
            q.nbias = sb(name + "_nbias", [P, LANES])
            q.moments, q.root, q.ready, q.applied, q.go = (
                sem(f"{name}_{n}") for n in ("moments", "root", "ready", "applied", "go"))
            return q

        b = Phase()
        phase_tiles()
        b.x, b.xT, b.agg = tile2(), tile2(), tile2()
        b.y, b.z = tile2(), tile()
        b.hT = tile2()
        b.small = [tile(), tile()]
        b.f = [tile(), tile()]
        b.y2T = tile()
        b.xb = tile2()
        b.z2 = tile()
        b.y3 = tile2()
        b.x1 = tile2()
        b.z4 = tile()
        b.h1T = tile()
        b.sq = tile()
        b.xl, b.xr = tile2(), tile2()
        b.ln = [stats_tiles(f"b_ln{k}") for k in range(4)]
        b.resid = sem("b_resid")
        b.skipped = sem("b_skipped")
        b.y_ready = sem("b_y_ready")
        b.turned1 = sem("b_turned1")
        b.h_ready = sem("b_h_ready")
        b.up = sem("b_up")
        b.small_up = sem("b_small_up")
        b.act_up = sem("b_act_up")
        b.down = sem("b_down")
        b.y2_ready = sem("b_y2_ready")
        b.turned2 = sem("b_turned2")
        b.y3_ready = sem("b_y3_ready")
        b.turned4 = sem("b_turned4")
        b.h1_ready = sem("b_h1_ready")
        b.squared = sem("b_squared")
        b.normed = sem("b_normed")
        b.lr = sem("b_lr")
        b.lr_ready = sem("b_lr_ready")
        b.hn_saved = sem("b_hn_saved")
        b.node_in = sem2("b_node_in")
        b.xb_in = sem2("b_xb_in")
        b.x1_out = sem2("b_x1_out")
        b.lr_out = sem2("b_lr_out")

        d = Phase()
        phase_tiles()
        d.x1, d.xl = tile2(), tile2()
        d.g = [tile(P, LANES * GROW), tile(P, LANES * GROW)]
        d.o, d.o2 = tile(), tile2()
        d.sq = tile()
        d.y = tile2()
        d.res = tile2()
        d.top = sb("d_top", [P, LANES * H1])
        d.ex = [sb(f"d_ex{k}", [P, 2, LANES * H1]) for k in range(2)]
        d.diff = sb("d_diff", [P, 2, LANES * H1])
        d.dn = sb("d_dn", [P, LANES * H1])
        d.ss = sb("d_ss", [P, LANES])
        d.nrm = sb("d_nrm", [P, LANES])
        d.fac = sb("d_fac", [P, LANES])
        d.ln = stats_tiles("d_ln")
        d.doubled = sem("d_doubled")
        d.top_ready = sem("d_top_ready")
        d.diffs = sem("d_diffs")
        d.exps = sem("d_exps")
        d.shares = sem("d_shares")
        d.part_e = sem("d_part_e")
        d.part_s = sem("d_part_s")
        d.sum_es = sem("d_sum_es")
        d.o_ready = sem("d_o_ready")
        d.sq_ready = sem("d_sq_ready")
        d.nrm_ready = sem("d_nrm_ready")
        d.fac_ready = sem("d_fac_ready")
        d.y_ready = sem("d_y_ready")
        d.g_in = sem2("d_g_in")
        d.xl_in = sem2("d_xl_in")
        d.x1_in = sem2("d_x1_in")
        d.out_done = sem2("d_out_done")

        def wait_prep(eng):
            eng.wait_ge(loaded, 16 * N_LOADS)
            eng.wait_ge(memset_done, 8)
            eng.wait_ge(prep_dve, 9)

        def wait_scatters(eng, q):
            for k in range(2):
                eng.wait_ge(q.scattered[k], 16 * LANES * BLOCKS // 2)

        def wait_node_stores(eng):
            for k in range(2):
                eng.wait_ge(b.x1_out[k], 16 * BLOCKS // 2)
                eng.wait_ge(b.lr_out[k], 32 * BLOCKS // 2)
            eng.wait_ge(b.hn_saved, BLOCKS)

        def heads(ap):
            return ap.rearrange("p (h e) -> p h e", e=C1)

        def wide(ap):
            return ap.unsqueeze(2).to_broadcast([P, LANES * H1, C1])

        def gsum(ap):
            return ap.rearrange("p (j f) -> p j f", j=LANES)[:, :, 0:P].rearrange("p j (h e) -> p j h e", e=C1)

        loads = [
            (ident[:, :], t["ident"]), (headmask[:, :], t["headmask"]), (headpick[:, :], t["headpick"]),
            (sumx[:, :, :], t["sumx"]), (sume[:, :], t["sume"]), (spread_w[:, :, :], t["spread_w"]),
            (wq[:, :, :], t["Wq"].rearrange("(h c) f -> c h f", h=H0)),
            (wk[:, :, :], t["Wk"].rearrange("(h c) f -> c h f", h=H0)),
            (wexb[:, :, :], t["wexb"]),
            (bq[:, :], t["bq"]),
            (wv[:, :, :], t["WvT"].rearrange("f (h c) -> f h c", h=H0)),
            (wve[:, :, :], t["wve"]),
            (wskip[:, :], t["WskipT"]),
            (w1[:, :, :], t["W1T"].rearrange("f (h c) -> f h c", h=2)),
            (w2[:, :, :], t["W2T"].rearrange("(h c) f -> c h f", h=2)),
            (wlr[:, 0, :], t["W_l"]), (wlr[:, 1, :], t["W_r"]),
            (cols[:, :], t["cols"]),
            (rows[:, :, :], t["rows"].partition_broadcast(P)),
            (scalec[:, :], t["scale"].partition_broadcast(P)),
            (dstrow[:, :, :], t["dstrow"]),
        ]
        N_LOADS = len(loads)

        block = ctx.enter_context(nc.Block())

        @block.sync
        def _(eng):
            for dst, src in loads:
                eng.dma_start(dst, src).then_inc(loaded, 16)
            eng.wait_ge(resets_done, 2)
            eng.dma_start(reset_d[:, :], resets[:, :]).then_inc(reset_stored, 16)
            eng.wait_ge(reset_stored, 16)

            def edge_indices(q, ends_lag, s):
                if active(s):
                    k = parity(s)
                    if since(s, 2):
                        eng.wait_ge(q.gathered[parity(back(s, 2))], slot(back(s, 2), 2 * 16 * LANES))
                    eng.dma_start(idx[k][:, :, :], t["idx"][bass.ds(at(s, 1), 1), :, 0:2, :].rearrange("a p v j -> (a p) v j")).then_inc(q.idx_in[k], 16)
                g = back(s, ends_lag)
                if active(g):
                    k = parity(g)
                    if since(g, 2):
                        eng.wait_ge(q.lastrow, total(back(g, 2), 2))
                    eng.dma_start(ends[k][:, :, :], t["idx"][bass.ds(at(g, 1), 1), :, 1:3, :].rearrange("a p v j -> (a p) v j")).then_inc(q.ends_in[k], 16)

            def a_step(s):
                edge_indices(a, 3, s)
                g = back(s, 1)
                if active(g):
                    k = parity(g)
                    if since(g, 2):
                        eng.wait_ge(a.shifts, total(back(g, 2), 3))
                    if since(g, 2):
                        eng.wait_ge(a.weighted, total(back(g, 2), 3))
                    eng.dma_start(a.reset[k], reset_d[bass.ds(at(g, 1), 1), :].partition_broadcast(ROWS_E)).then_inc(a.edge_in[k], 16)
                    for h in range(H0):
                        eng.dma_start(a.ext[k][h * EDIM:(h + 1) * EDIM, :], t["eaT"][:, bass.ds(at(g, W), W)]).then_inc(a.edge_in[k], 16)
            steps(eng, A_LAGS, a_step, unroll=2)

            wait_scatters(eng, a)

            def b_step(s):
                if active(s):
                    k = parity(s)
                    if since(s, 2):
                        eng.wait_ge(b.resid, total(back(s, 2), 2))
                        eng.wait_ge(b.skipped, total(back(s, 2), 1))
                        eng.wait_ge(b.y_ready, total(back(s, 2), 1))
                    r = bass.ds(at(s, W), W)
                    eng.dma_start(b.x[k], t["x"][r, :].rearrange("(p j) f -> p (j f)", p=P)).then_inc(b.node_in[k], 16)
                    eng.dma_start(b.xT[k], t["xT"][:, r]).then_inc(b.node_in[k], 16)
                    eng.dma_start(b.agg[k], agg_d[r, :].rearrange("(p j) f -> p (j f)", p=P)).then_inc(b.node_in[k], 16)
                g = back(s, 4)
                if active(g):
                    k = parity(g)
                    if since(g, 2):
                        eng.wait_ge(b.y3_ready, total(back(g, 2), 3))
                    eng.dma_start(b.xb[k], t["x"][bass.ds(at(g, W), W), :].rearrange("(p j) f -> p (j f)", p=P)).then_inc(b.xb_in[k], 16)
                g = back(s, 6)
                if active(g):
                    k = parity(g)
                    eng.wait_ge(b.ln[2].applied, total(g, LANES))
                    eng.dma_start(x1_d[bass.ds(at(g, W), W), :].rearrange("(p j) f -> p (j f)", p=P), b.x1[k]).then_inc(b.x1_out[k], 16)
                g = back(s, 8)
                if active(g):
                    k = parity(g)
                    r = bass.ds(at(g, W), W)
                    eng.wait_ge(b.lr_ready, total(g, 2))
                    eng.dma_start(xl_d[r, :].rearrange("(p j) f -> p (j f)", p=P), b.xl[k]).then_inc(b.lr_out[k], 16)
                    eng.dma_start(xr_d[r, :].rearrange("(p j) f -> p (j f)", p=P), b.xr[k]).then_inc(b.lr_out[k], 16)
            steps(eng, B_LAGS, b_step, unroll=2)

            wait_node_stores(eng)

            def c_step(s):
                edge_indices(c, 2, s)
                if active(s):
                    k = parity(s)
                    if since(s, 2):
                        eng.wait_ge(c.self_scored, total(back(s, 2), 4))
                    r = bass.ds(at(s, W), W)
                    eng.dma_start(c.own_l[k], xl_d[r, :].rearrange("(p j) f -> p (j f)", p=P)).then_inc(c.own_in[k], 16)
                    eng.dma_start(c.own_r[k], xr_d[r, :].rearrange("(p j) f -> p (j f)", p=P)).then_inc(c.own_in[k], 16)
                g = back(s, 1)
                if active(g):
                    k = parity(g)
                    if since(g, 2):
                        eng.wait_ge(c.shifts, total(back(g, 2), 3))
                    eng.dma_start(c.reset[k], reset_d[bass.ds(at(g, 1), 1), :].partition_broadcast(P)).then_inc(c.edge_in[k], 16)
            steps(eng, C_LAGS, c_step, unroll=2)

            wait_scatters(eng, c)

            def d_step(s):
                g = back(s, 1)
                if active(g):
                    k = parity(g)
                    if since(g, 2):
                        eng.wait_ge(d.part_s, total(back(g, 2), 1))
                    eng.dma_start(d.xl[k], xl_d[bass.ds(at(g, W), W), :].rearrange("(p j) f -> p (j f)", p=P)).then_inc(d.xl_in[k], 16)
                g = back(s, 2)
                if active(g):
                    k = parity(g)
                    if since(g, 2):
                        eng.wait_ge(d.y_ready, total(back(g, 2), LANES))
                    eng.dma_start(d.x1[k], x1_d[bass.ds(at(g, W), W), :].rearrange("(p j) f -> p (j f)", p=P)).then_inc(d.x1_in[k], 16)
                g = back(s, 5)
                if active(g):
                    k = parity(g)
                    eng.wait_ge(d.ln.applied, total(g, LANES))
                    eng.dma_start(out[bass.ds(at(g, W), W), :].rearrange("(p j) f -> p (j f)", p=P), d.res[k]).then_inc(d.out_done[k], 16)
                if active(s):
                    k = parity(s)
                    if since(s, 2):
                        eng.wait_ge(d.part_e, total(back(s, 2), 1))
                    eng.dma_start(d.g[k], gat_d[bass.ds(at(s, W), W), :].rearrange("(p j) f -> p (j f)", p=P)).then_inc(d.g_in[k], 16)
            steps(eng, D_LAGS, d_step, unroll=2)
            for k in range(2):
                eng.wait_ge(d.out_done[k], 16 * BLOCKS // 2)

        @block.gpsimd
        def _(eng):
            wait_prep(eng)
            def edge_step(q, tab_s, tab_d, buf_s, buf_d, node_table, row_buf, row_width, scatter_lag, s):
                if active(s):
                    k = parity(s)
                    eng.wait_ge(q.idx_in[parity(s)], slot(s, 16))
                    if since(s, 2):
                        eng.wait_ge(q.turned, total(back(s, 2), 2))
                    eng.sem_inc(q.go, 1)
                    for tab, buf, v in ((tab_s, buf_s, 0), (tab_d, buf_d, 1)):
                        for j in range(LANES):
                            eng.indirect_dma_start(
                                buf[k][:, j * P:(j + 1) * P], None, tab[:, :],
                                bass.IndirectOffsetOnAxis(ap=idx[k][:, v, j:j + 1].bitcast(U32), axis=0),
                            ).then_inc(q.gathered[k], 16)
                g = back(s, scatter_lag)
                if active(g):
                    k = parity(g)
                    eng.wait_ge(q.done_rows, total(g, q.rows_per_block))
                    eng.wait_ge(q.lastrow, total(g, 2))
                    if static(g) and g[1] == 0:
                        eng.wait_ge(q.filled, 16 * q.fills)
                    eng.sem_inc(q.go, 1)
                    for j in range(LANES):
                        eng.indirect_dma_start(
                            node_table[:, :],
                            bass.IndirectOffsetOnAxis(ap=last[k][:, j:j + 1].bitcast(U32), axis=0),
                            row_buf[k][:, j * row_width:(j + 1) * row_width], None,
                            bounds_check=NP - 1, oob_is_err=False,
                        ).then_inc(q.scattered[k], 16)

            a.done_rows, a.rows_per_block, a.fills = a.combined, LANES, NP // (FILL * P)
            steps(eng, A_LAGS, lambda s: edge_step(a, t["x"], t["x"], a.xs, a.xd, agg_d, a.agg, P, A_LAGS, s))
            for k in range(2):
                eng.wait_ge(a.scattered[k], 16 * LANES * BLOCKS // 2)

            def b_step(s):
                g = back(s, 1)
                if active(g):
                    k = parity(g)
                    eng.wait_ge(b.node_in[k], slot(g, 48))
                    eng.tensor_tensor(lanes(b.agg[k]), lanes(b.agg[k]), rows[:, 0:1, :].to_broadcast([P, LANES, P]), ALU.add).then_inc(b.resid, 1)
                    eng.wait_ge(b.resid, part(g, 2, 1))
                    eng.tensor_tensor(b.agg[k], b.agg[k], b.x[k], ALU.add).then_inc(b.resid, 1)
                g = back(s, 5)
                if active(g):
                    k = parity(g)
                    eng.wait_ge(b.ln[1].applied, total(g, LANES))
                    if since(g, 2):
                        eng.wait_ge(b.ln[2].applied, total(back(g, 2), LANES))
                    eng.tensor_tensor(lanes(b.y3[k]), lanes(b.z2), rows[:, 1:2, :].to_broadcast([P, LANES, P]), ALU.mult).then_inc(b.y3_ready, 1)
                    eng.wait_ge(b.xb_in[k], slot(g, 16))
                    eng.tensor_tensor(lanes(b.xb[k]), lanes(b.xb[k]), rows[:, 2:3, :].to_broadcast([P, LANES, P]), ALU.add).then_inc(b.y3_ready, 1)
                    eng.wait_ge(b.y3_ready, part(g, 3, 2))
                    eng.tensor_tensor(b.y3[k], b.y3[k], b.xb[k], ALU.add).then_inc(b.y3_ready, 1)
            steps(eng, B_LAGS, b_step)
            wait_node_stores(eng)

            c.done_rows, c.rows_per_block, c.fills = c.packed, 2, BLOCKS
            steps(eng, C_LAGS, lambda s: edge_step(c, xl_d, xr_d, c.xl, c.xr, gat_d, c.row, GROW, C_LAGS, s))
            wait_scatters(eng, c)

            def d_step(s):
                g = back(s, 3)
                if active(g):
                    k = parity(g)
                    eng.wait_ge(d.x1_in[k], slot(g, 16))
                    eng.tensor_tensor(d.x1[k], d.x1[k], d.x1[k], ALU.add).then_inc(d.doubled, 1)
                g = back(s, 2)
                if active(g):
                    k = parity(g)
                    eng.wait_ge(d.shares, total(g, 4))
                    if since(g, 1):
                        eng.wait_ge(d.sum_es, total(back(g, 1), 1))
                    eng.tensor_tensor(heads(d.o), gsum(d.g[k]), wide(d.ex[k][:, 0, :]), ALU.mult).then_inc(d.part_e, 1)
                g = back(s, 2)
                if active(g):
                    k = parity(g)
                    eng.wait_ge(d.sum_es, total(g, 1))
                    eng.tensor_tensor(lanes(d.o2[k]), lanes(d.o2[k]), rows[:, 6:7, :].to_broadcast([P, LANES, P]), ALU.add).then_inc(d.o_ready, 1)
            steps(eng, D_LAGS, d_step)

        def statistics(eng, ln, src, g):
            if since(g, 1):
                eng.wait_ge(ln.moments, total(back(g, 1), 2 * LANES))
            for j in range(LANES):
                eng.bn_stats(ln.stats[:, j, :], src[:, j * P:(j + 1) * P]).then_inc(ln.moments, 1)

        def aggregate(eng, ln, g):
            eng.wait_ge(ln.moments, part(g, 2 * LANES, LANES))
            if since(g, 1):
                eng.wait_ge(ln.root, total(back(g, 1), 1))
                eng.wait_ge(ln.ready, total(back(g, 1), 2))
            eng.sem_inc(ln.go, 1)
            for j in range(LANES):
                eng.bn_aggr(ln.mv[:, j, :], ln.stats[:, j, :]).then_inc(ln.moments, 1)

        def reciprocals(eng, ln, g):
            if since(g, 1):
                eng.wait_ge(ln.applied, total(back(g, 1), LANES))
            eng.wait_ge(ln.moments, total(g, 2 * LANES))
            eng.wait_ge(ln.root, total(g, 1))
            eng.reciprocal(ln.rstd[:, :], ln.sd[:, :]).then_inc(ln.ready, 1)

        def offsets(eng, ln, g):
            eng.wait_ge(ln.ready, part(g, 2, 1))
            eng.scalar_tensor_tensor(out=ln.nbias[:, :], in0=ln.mv[:, :, 0], scalar=-1.0, in1=ln.rstd[:, :],
                                     op0=ALU.mult, op1=ALU.mult).then_inc(ln.ready, 1)

        def root(eng, ln, g):
            eng.wait_ge(ln.moments, total(g, 2 * LANES))
            if since(g, 1):
                eng.wait_ge(ln.ready, total(back(g, 1), 2))
            eng.activation(ln.sd[:, :], ln.mv[:, :, 1], ACT.Sqrt, bias=epsc[:, 0:1]).then_inc(ln.root, 1)

        def normalise(eng, ln, src, dst, g):
            eng.wait_ge(ln.ready, total(g, 2))
            for j in range(LANES):
                eng.activation(dst[:, j * P:(j + 1) * P], src[:, j * P:(j + 1) * P], ACT.Identity,
                               bias=ln.nbias[:, j:j + 1], scale=ln.rstd[:, j:j + 1]).then_inc(ln.applied, 1)

        def find_last(eng, q, g):
            k = parity(g)
            eng.wait_ge(q.ends_in[parity(g)], slot(g, 16))
            if since(g, 1):
                eng.wait_ge(q.lastrow, total(back(g, 1), 2))
            if since(g, 2):
                eng.wait_ge(q.scattered[parity(back(g, 2))], slot(back(g, 2), 16 * LANES))
            eng.tensor_tensor(lastf[:, :], ends[k][:, 0, :], ends[k][:, 1, :], ALU.is_equal).then_inc(q.lastrow, 1)
            eng.wait_ge(q.lastrow, part(g, 2, 1))
            eng.scalar_tensor_tensor(out=last[k][:, :], in0=lastf[:, :], scalar=float(SKIP), in1=ends[k][:, 0, :],
                                     op0=ALU.mult, op1=ALU.add).then_inc(q.lastrow, 1)

        def run_maxima(eng, q, score, n, g):
            k = parity(g)
            o = k * W
            if k == 0:
                if since(g, 1):
                    eng.wait_ge(q.maxima, total(back(g, 1), 1))
                q.free_maxima(eng, g)
                eng.tensor_copy(q.runmax[:, 0:1], q.runmax[:, 2 * W:2 * W + 1]).then_inc(q.carried, 1)
                eng.wait_ge(q.carried, g[0] + g[1] // 2 + 1)
            eng.wait_ge(q.scored, total(g, q.scores_per_block))
            eng.wait_ge(q.edge_in[parity(g)], slot(g, q.edge_loads))
            if since(g, 1):
                eng.wait_ge(q.maxima, total(back(g, 1), 1))
            if since(g, 1):
                eng.wait_ge(q.shifts, total(back(g, 1), 3))
            if k == 1:
                q.free_maxima(eng, g)
            eng.tensor_tensor_scan(q.runmax[:, o + 1:o + W + 1], q.reset[k], score, q.runmax[:, o:o + 1],
                                   ALU.add, ALU.max).then_inc(q.maxima, 1)
            eng.wait_ge(q.maxima, total(g, 1))
            if since(g, 1):
                eng.wait_ge(q.weights, total(back(g, 1), 1))
            eng.tensor_tensor(q.shift[:, 0:W], score, q.runmax[:, o + 1:o + W + 1], ALU.subtract).then_inc(q.shifts, 1)
            eng.tensor_tensor(q.shift[:, W:2 * W], q.runmax[:, o:o + W], q.runmax[:, o + 1:o + W + 1], ALU.subtract).then_inc(q.shifts, 1)
            eng.wait_ge(q.shifts, part(g, 3, 2))
            eng.tensor_tensor(q.shift[:, W:2 * W], q.shift[:, W:2 * W], q.reset[k], ALU.add).then_inc(q.shifts, 1)

        @block.vector
        def _(eng):
            eng.memset(zeros[:, :, :], 0.0).then_inc(memset_done, 1)
            eng.memset(fill[:, :, 0:P + H1], 0.0).then_inc(memset_done, 1)
            eng.memset(fill[:, :, P + H1:GROW], FAR).then_inc(memset_done, 1)
            eng.memset(ones[:, :], 1.0).then_inc(memset_done, 1)
            eng.memset(epsc[:, :], EPS).then_inc(memset_done, 1)
            for k in range(2):
                eng.memset(a.ext[k][DEN0:ROWS_E, :], 1.0).then_inc(memset_done, 1)
            eng.memset(a.runmax[:, :], 0.0).then_inc(memset_done, 1)
            eng.wait_ge(loaded, 16 * N_LOADS)
            eng.tensor_tensor(resets[:, :], dstrow[:, 0, :], dstrow[:, 1, :], ALU.not_equal).then_inc(resets_done, 1)
            eng.wait_ge(resets_done, 1)
            eng.tensor_scalar(resets[:, :], resets[:, :], FAR, None, ALU.mult).then_inc(resets_done, 1)
            eng.wait_ge(prep_mm, 6)
            for h in range(H0):
                eng.tensor_copy(qk[:, h, :], bank[h][:, 0:P]).then_inc(prep_dve, 1)
                eng.tensor_copy(ck[:, h:h + 1], bank[2 + h][:, 0:1]).then_inc(prep_dve, 1)
            eng.tensor_copy(qe[:, :], bank[4][:, 0:ROWS_E]).then_inc(prep_dve, 1)
            eng.tensor_copy(ce[:, :], bank[5][0:ROWS_E, 0:1]).then_inc(prep_dve, 1)
            eng.tensor_scalar(attb[:, :], headmask[:, :], cols[:, 7:8], None, ALU.mult).then_inc(prep_dve, 1)
            eng.tensor_scalar(b1s[:, :], cols[:, 0:2], 0.01, None, ALU.mult).then_inc(prep_dve, 1)
            eng.memset(lastf[:, :], 0.0).then_inc(prep_dve, 1)
            wait_prep(eng)
            a.free_maxima = lambda e, g: None
            a.scores_per_block, a.edge_loads = 1, 48

            def a_step(s):
                g = back(s, 4)
                if active(g):
                    k = parity(g)
                    for pair in range(LANES // 2):
                        for j in (2 * pair, 2 * pair + 1):
                            eng.wait_ge(a.values, part(g, LANES, j + 1))
                            if since(g, 1):
                                eng.wait_ge(a.denoms, total(back(g, 1), 6))
                            eng.tensor_scalar(a.den[:, j, :], value_bank[j][:, P:2 * VCOL:VCOL], float(H0), H0 * 1e-16, ALU.mult, ALU.add).then_inc(a.denoms, 1)
                        eng.wait_ge(a.denoms, part(g, 6, 3 * pair + 2))
                        if since(g, 1):
                            eng.wait_ge(a.combined, total(back(g, 1), LANES))
                        eng.reciprocal(a.rden[:, 2 * pair:2 * pair + 2, :], a.den[:, 2 * pair:2 * pair + 2, :]).then_inc(a.denoms, 1)
                        for j in (2 * pair, 2 * pair + 1):
                            o = a.agg[k][:, j * P:(j + 1) * P]
                            eng.wait_ge(a.head0, part(g, LANES, j + 1))
                            eng.wait_ge(a.denoms, part(g, 6, 3 * pair + 3))
                            eng.scalar_tensor_tensor(out=o, in0=value_bank[j][:, VCOL:VCOL + P], scalar=a.rden[:, j, 1:2],
                                                     in1=o, op0=ALU.mult, op1=ALU.add).then_inc(a.combined, 1)
                g = back(s, 2)
                if active(g):
                    k = parity(g)
                    eng.wait_ge(a.evacuated, total(g, 2))
                    eng.wait_ge(a.edge_in[k], slot(g, 48))
                    if since(g, 1):
                        eng.wait_ge(a.scored, total(back(g, 1), 1))
                    for h in range(H0):
                        eng.wait_ge(a.projected, part(g, 3, h + 1))
                        eng.scalar_tensor_tensor(out=a.prod[h], in0=bank[2 + h][:, :], scalar=ck[:, h:h + 1], in1=a.xsT[k],
                                                 op0=ALU.add, op1=ALU.mult).then_inc(a.products, 1)
                def running_sum(g, h):
                    k = parity(g)
                    eng.wait_ge(a.spread, part(g, 4, 2 * h + 1))
                    eng.tensor_tensor(a.pv[h], bank[6][:, :], a.xsT[k], ALU.mult).then_inc(a.weighted, 1)
                    eng.wait_ge(a.spread, part(g, 4, 2 * h + 2))
                    eng.wait_ge(a.weighted, part(g, 3, h + 1))
                    if since(g, 2):
                        eng.wait_ge(a.values, total(back(g, 2), LANES))
                    if since(g, 1):
                        eng.wait_ge(a.summed, total(back(g, 1), 3))
                    first = 0.0 if static(g) and g[1] == 0 else a.num[h][1 - k][:, W - 1:W]
                    eng.tensor_tensor_scan(a.num[h][k], bank[7][:, :], a.pv[h], first, ALU.mult, ALU.add).then_inc(a.summed, 1)

                g = back(s, 3)
                if active(g):
                    running_sum(g, 0)
                g = back(s, 2)
                if active(g):
                    k = parity(g)
                    eng.wait_ge(a.projected, total(g, 3))
                    eng.scalar_tensor_tensor(out=a.prode, in0=bank[4][0:ROWS_E, :], scalar=ce[:, 0:1], in1=a.ext[k],
                                             op0=ALU.add, op1=ALU.mult).then_inc(a.products, 1)
                g = back(s, 3)
                if active(g):
                    k = parity(g)
                    running_sum(g, 1)
                    eng.tensor_tensor(a.pve, a.pd[k][:, 0:W], a.ext[k], ALU.mult).then_inc(a.weighted, 1)
                    eng.wait_ge(a.weighted, total(g, 3))
                    first = 0.0 if static(g) and g[1] == 0 else a.nume[1 - k][:, W - 1:W]
                    eng.tensor_tensor_scan(a.nume[k], a.pd[k][:, W:2 * W], a.pve, first, ALU.mult, ALU.add).then_inc(a.summed, 1)
                g = back(s, 2)
                if active(g):
                    run_maxima(eng, a, bank[5][0:ROWS_E, :], ROWS_E, g)
                g = back(s, 4)
                if active(g):
                    find_last(eng, a, g)
            steps(eng, A_LAGS, a_step)
            wait_scatters(eng, a)

            def b_step(s):
                g = back(s, 4)
                if active(g):
                    eng.wait_ge(b.turned2, total(g, 1))
                    statistics(eng, b.ln[1], y2_bank[parity(g)], g)
                g = back(s, 1)
                if active(g):
                    k = parity(g)
                    eng.wait_ge(b.skipped, total(g, 1))
                    eng.wait_ge(b.resid, total(g, 2))
                    if since(g, 2):
                        eng.wait_ge(b.ln[0].applied, total(back(g, 2), LANES))
                    eng.tensor_tensor(b.y[k], bank[1][:, :], b.agg[k], ALU.add).then_inc(b.y_ready, 1)
                g = back(s, 4)
                if active(g):
                    aggregate(eng, b.ln[1], g)
                g = back(s, 1)
                if active(g):
                    eng.wait_ge(b.y_ready, total(g, 1))
                    statistics(eng, b.ln[0], b.y[parity(g)], g)
                g = back(s, 1)
                if active(g):
                    aggregate(eng, b.ln[0], g)
                g = back(s, 6)
                if active(g):
                    eng.wait_ge(b.ln[2].applied, total(g, LANES))
                    statistics(eng, b.ln[3], b.x1[parity(g)], g)
                g = back(s, 1)
                if active(g):
                    reciprocals(eng, b.ln[0], g)
                g = back(s, 1)
                if active(g):
                    offsets(eng, b.ln[0], g)
                g = back(s, 4)
                if active(g):
                    reciprocals(eng, b.ln[1], g)
                g = back(s, 6)
                if active(g):
                    aggregate(eng, b.ln[3], g)
                g = back(s, 5)
                if active(g):
                    eng.wait_ge(b.y3_ready, total(g, 3))
                    statistics(eng, b.ln[2], b.y3[parity(g)], g)
                g = back(s, 4)
                if active(g):
                    offsets(eng, b.ln[1], g)
                g = back(s, 5)
                if active(g):
                    aggregate(eng, b.ln[2], g)
                g = back(s, 3)
                if active(g):
                    k = parity(g)
                    eng.wait_ge(b.down, total(g, 1))
                    if since(g, 1):
                        eng.wait_ge(b.turned2, total(back(g, 1), 1))
                    eng.scalar_tensor_tensor(out=b.y2T, in0=bank[4][:, :], scalar=cols[:, 2:3], in1=b.hT[k],
                                             op0=ALU.add, op1=ALU.add).then_inc(b.y2_ready, 1)
                g = back(s, 6)
                if active(g):
                    reciprocals(eng, b.ln[3], g)
                g = back(s, 5)
                if active(g):
                    reciprocals(eng, b.ln[2], g)
                g = back(s, 7)
                if active(g):
                    k = parity(g)
                    for n, dst in enumerate((b.xl[k], b.xr[k])):
                        eng.wait_ge(b.lr, part(g, 2, n + 1))
                        if since(g, 2):
                            eng.wait_ge(b.lr_out[k], slot(back(g, 2), 32))
                        eng.tensor_tensor(lanes(dst), lanes(bank[6 + n][:, :]), rows[:, 3 + n:4 + n, :].to_broadcast([P, LANES, P]), ALU.add).then_inc(b.lr_ready, 1)
                g = back(s, 7)
                if active(g):
                    eng.wait_ge(b.normed, total(g, 1))
                    eng.tensor_copy(hnorm[:, bass.ds(at(g, 1), 1), :].rearrange("p a j -> p (a j)"), bank[1][:, 0:LANES]).then_inc(b.hn_saved, 1)
                g = back(s, 6)
                if active(g):
                    offsets(eng, b.ln[3], g)
                g = back(s, 5)
                if active(g):
                    offsets(eng, b.ln[2], g)
                g = back(s, 2)
                if active(g):
                    for h in range(2):
                        eng.wait_ge(b.small_up, part(g, 2, h + 1))
                        if since(g, 1):
                            eng.wait_ge(b.down, total(back(g, 1), 1))
                        eng.scalar_tensor_tensor(out=b.f[h], in0=bank[3 - h][:, :], scalar=cols[:, h:h + 1], in1=b.small[h],
                                                 op0=ALU.add, op1=ALU.max).then_inc(b.act_up, 1)
            steps(eng, B_LAGS, b_step)
            wait_node_stores(eng)
            eng.memset(c.runmax[:, 2 * W:2 * W + 1], 0.0).then_inc(prep_dve, 1)
            eng.wait_ge(prep_dve, 10)

            def c_free(e, g):
                if since(g, 2):
                    e.wait_ge(c.returned, total(back(g, 2), 2))
            c.free_maxima = c_free
            c.scores_per_block, c.edge_loads = 1, 16

            def c_step(s):
                g = back(s, 2)
                if active(g):
                    k = parity(g)
                    eng.wait_ge(c.turned, total(g, 2))
                    eng.wait_ge(c.evacuated, total(g, 1))
                    if since(g, 1):
                        eng.wait_ge(c.feats, total(back(g, 1), 2))
                    eng.tensor_tensor(c.z, bank[1][:, :], c.xlT[k], ALU.add).then_inc(c.feats, 1)
                    eng.wait_ge(c.feats, part(g, 2, 1))
                    if since(g, 1):
                        eng.wait_ge(c.scored, total(back(g, 1), 1))
                    eng.scalar_tensor_tensor(out=c.leaky, in0=c.z, scalar=0.2, in1=c.z, op0=ALU.mult, op1=ALU.max).then_inc(c.feats, 1)
                g = back(s, 3)
                if active(g):
                    k = parity(g)
                    eng.wait_ge(c.weights, total(g, 1))
                    eng.tensor_tensor(c.pv, c.pd[k][:, 0:W], c.xlT[k], ALU.mult).then_inc(c.weighted, 1)
                    if since(g, 2):
                        eng.wait_ge(c.returned, total(back(g, 2), 2))
                    if since(g, 1):
                        eng.wait_ge(c.summed, total(back(g, 1), 2))
                    start = static(g) and g[1] == 0
                    eng.tensor_tensor_scan(c.den[k], c.pd[k][:, W:2 * W], c.pd[k][:, 0:W],
                                           0.0 if start else c.den[1 - k][:, W - 1:W], ALU.mult, ALU.add).then_inc(c.summed, 1)
                    eng.wait_ge(c.weighted, total(g, 1))
                    eng.tensor_tensor_scan(c.num[k], c.pd[k][:, W:2 * W], c.pv,
                                           0.0 if start else c.num[1 - k][:, W - 1:W], ALU.mult, ALU.add).then_inc(c.summed, 1)
                g = back(s, 2)
                if active(g):
                    run_maxima(eng, c, bank[2][:, :], P, g)
                g = back(s, 3)
                if active(g):
                    k = parity(g)
                    find_last(eng, c, g)
                    eng.wait_ge(c.returned, total(g, 2))
                    eng.tensor_copy(c.row[k].rearrange("p (j f) -> p j f", j=LANES)[:, :, P:GROW],
                                    bank[4][:, 0:LANES * 2 * H1].rearrange("p (j f) -> p j f", j=LANES)).then_inc(c.packed, 1)
                g = back(s, 1)
                if active(g):
                    k = parity(g)
                    eng.wait_ge(c.own_in[k], slot(g, 32))
                    if since(g, 1):
                        eng.wait_ge(c.self_scored, total(back(g, 1), 4))
                    eng.tensor_tensor(c.own_z, c.own_l[k], c.own_r[k], ALU.add).then_inc(c.self_scored, 1)
                    eng.wait_ge(c.self_scored, part(g, 4, 1))
                    eng.scalar_tensor_tensor(out=c.own_z, in0=c.own_z, scalar=0.2, in1=c.own_z, op0=ALU.mult, op1=ALU.max).then_inc(c.self_scored, 1)
                    eng.wait_ge(c.self_scored, part(g, 4, 2))
                    eng.tensor_tensor(lanes(c.own_z), lanes(c.own_z), rows[:, 5:6, :].to_broadcast([P, LANES, P]), ALU.mult).then_inc(c.self_scored, 1)
                    eng.wait_ge(c.self_scored, part(g, 4, 3))
                    eng.tensor_reduce(selfs[:, bass.ds(at(g, 1), 1), :].rearrange("p a n -> p (a n)"), heads(c.own_z), AX.X, ALU.add).then_inc(c.self_scored, 1)
            steps(eng, C_LAGS, c_step)
            wait_scatters(eng, c)

            eng.wait_ge(hnorm_ready, 1)
            eng.wait_ge(c.self_scored, 4 * BLOCKS)

            def gcols(ap, first):
                return ap.rearrange("p (j f) -> p j f", j=LANES)[:, :, P + first:P + first + H1]

            def jh(ap):
                return ap.rearrange("p (j h) -> p j h", j=LANES)

            def d_step(s):
                g = back(s, 2)
                if active(g):
                    k = parity(g)
                    eng.wait_ge(d.exps, total(g, 1))
                    if since(g, 1):
                        eng.wait_ge(d.shares, total(back(g, 1), 4))
                    eng.tensor_tensor(jh(d.dn[:, :]), gcols(d.g[k], 0), jh(d.ex[k][:, 0, :]), ALU.mult).then_inc(d.shares, 1)
                    eng.wait_ge(d.shares, part(g, 4, 1))
                    eng.tensor_tensor(d.dn[:, :], d.dn[:, :], d.ex[k][:, 1, :], ALU.add).then_inc(d.shares, 1)
                g = back(s, 1)
                if active(g):
                    k = parity(g)
                    own = selfs[:, bass.ds(at(g, 1), 1), :].rearrange("p a n -> p (a n)")
                    eng.wait_ge(d.g_in[k], slot(g, 16))
                    if since(g, 1):
                        eng.wait_ge(d.diffs, total(back(g, 1), 2))
                    eng.tensor_tensor(jh(d.top[:, :]), gcols(d.g[k], H1), jh(own), ALU.max).then_inc(d.top_ready, 1)
                g = back(s, 2)
                if active(g):
                    k = parity(g)
                    eng.wait_ge(d.shares, part(g, 4, 2))
                    eng.reciprocal(d.dn[:, :], d.dn[:, :]).then_inc(d.shares, 1)
                    eng.wait_ge(d.shares, part(g, 4, 3))
                    eng.tensor_tensor(d.ex[k][:, :, :], d.ex[k][:, :, :], d.dn[:, :].unsqueeze(1).to_broadcast([P, 2, LANES * H1]), ALU.mult).then_inc(d.shares, 1)
                g = back(s, 1)
                if active(g):
                    k = parity(g)
                    own = selfs[:, bass.ds(at(g, 1), 1), :].rearrange("p a n -> p (a n)")
                    eng.wait_ge(d.top_ready, total(g, 1))
                    if since(g, 1):
                        eng.wait_ge(d.exps, total(back(g, 1), 1))
                    eng.tensor_tensor(jh(d.diff[:, 0, :]), gcols(d.g[k], H1), jh(d.top[:, :]), ALU.subtract).then_inc(d.diffs, 1)
                    eng.tensor_tensor(d.diff[:, 1, :], own, d.top[:, :], ALU.subtract).then_inc(d.diffs, 1)
                g = back(s, 2)
                if active(g):
                    k = parity(g)
                    eng.wait_ge(d.shares, total(g, 4))
                    eng.wait_ge(d.xl_in[k], slot(g, 16))
                    if since(g, 2):
                        eng.wait_ge(d.sq_ready, total(back(g, 2), LANES))
                        eng.wait_ge(d.y_ready, total(back(g, 2), LANES))
                    eng.tensor_tensor(heads(d.o2[k]), heads(d.xl[k]), wide(d.ex[k][:, 1, :]), ALU.mult).then_inc(d.part_s, 1)
                g = back(s, 4)
                if active(g):
                    reciprocals(eng, d.ln, g)
                g = back(s, 3)
                if active(g):
                    eng.wait_ge(d.nrm_ready, total(g, 1))
                    if since(g, 1):
                        eng.wait_ge(d.y_ready, total(back(g, 1), LANES))
                    eng.tensor_scalar(d.fac[:, :], d.nrm[:, :], 1e-12, None, ALU.max).then_inc(d.fac_ready, 1)
                g = back(s, 4)
                if active(g):
                    offsets(eng, d.ln, g)
                g = back(s, 3)
                if active(g):
                    eng.wait_ge(d.fac_ready, part(g, 3, 1))
                    eng.reciprocal(d.fac[:, :], d.fac[:, :]).then_inc(d.fac_ready, 1)
                g = back(s, 2)
                if active(g):
                    k = parity(g)
                    eng.wait_ge(d.part_s, total(g, 1))
                    eng.wait_ge(d.part_e, total(g, 1))
                    eng.tensor_tensor(d.o2[k], d.o2[k], d.o, ALU.add).then_inc(d.sum_es, 1)
                g = back(s, 3)
                if active(g):
                    eng.wait_ge(d.fac_ready, part(g, 3, 2))
                    eng.scalar_tensor_tensor(out=d.fac[:, :], in0=d.fac[:, :], scalar=scalec[:, 0:1], in1=hnorm[:, bass.ds(at(g, 1), 1), :].rearrange("p a j -> p (a j)"),
                                             op0=ALU.mult, op1=ALU.mult).then_inc(d.fac_ready, 1)
                g = back(s, 3)
                if active(g):
                    k = parity(g)
                    eng.wait_ge(d.fac_ready, total(g, 3))
                    eng.wait_ge(d.doubled, total(g, 1))
                    if since(g, 2):
                        eng.wait_ge(d.ln.applied, total(back(g, 2), LANES))
                    for j in range(LANES):
                        q = slice(j * P, (j + 1) * P)
                        eng.scalar_tensor_tensor(out=d.y[k][:, q], in0=d.o2[k][:, q], scalar=d.fac[:, j:j + 1], in1=d.x1[k][:, q],
                                                 op0=ALU.mult, op1=ALU.add).then_inc(d.y_ready, 1)
                g = back(s, 3)
                if active(g):
                    k = parity(g)
                    eng.wait_ge(d.y_ready, total(g, LANES))
                    statistics(eng, d.ln, d.y[k], g)
                    aggregate(eng, d.ln, g)
            steps(eng, D_LAGS, d_step)

        @block.scalar
        def _(eng):
            eng.wait_ge(memset_done, 8)
            for k in range(NP // (FILL * P)):
                r = slice(k * FILL * P, (k + 1) * FILL * P)
                eng.dma_start(agg_d[r, :].rearrange("(p r) f -> p r f", p=P), zeros[:, :, :]).then_inc(a.filled, 16)
            wait_prep(eng)
            score_scale = float(P) ** -0.5

            def a_step(s):
                g = back(s, 2)
                if active(g):
                    eng.dma_start(gat_d[bass.ds(at(g, W), W), :].rearrange("(p r) f -> p r f", p=P), fill[:, :, :]).then_inc(c.filled, 16)
                g = back(s, 4)
                if active(g):
                    k = parity(g)
                    if since(g, 2):
                        eng.wait_ge(a.scattered[k], slot(back(g, 2), 16 * LANES))
                    for j in range(LANES):
                        eng.wait_ge(a.denoms, part(g, 6, 3 * (j // 2) + 3))
                        eng.activation(a.agg[k][:, j * P:(j + 1) * P], value_bank[j][:, 0:P], ACT.Copy,
                                       scale=a.rden[:, j, 0:1]).then_inc(a.head0, 1)
                g = back(s, 1)
                if active(g):
                    k = parity(g)
                    if since(g, 2):
                        eng.wait_ge(a.weighted, part(back(g, 2), 3, 2))
                        eng.wait_ge(a.projected, total(back(g, 2), 3))
                    eng.wait_ge(a.turned, part(g, 2, 1))
                    eng.activation(a.xsT[k], bank[0][:, :], ACT.Copy).then_inc(a.evacuated, 1)
                    eng.wait_ge(a.turned, total(g, 2))
                    eng.activation(a.xdT[k], bank[1][:, :], ACT.Copy).then_inc(a.evacuated, 1)
                g = back(s, 2)
                if active(g):
                    k = parity(g)
                    eng.wait_ge(a.shifts, total(g, 3))
                    if since(g, 2):
                        eng.wait_ge(a.summed, total(back(g, 2), 3))
                        eng.wait_ge(a.spread, total(back(g, 2), 4))
                    eng.activation(a.pd[k], a.shift, ACT.Exp, scale=score_scale).then_inc(a.weights, 1)
            steps(eng, A_LAGS, a_step)
            wait_scatters(eng, a)

            def b_step(s):
                g = back(s, 4)
                if active(g):
                    root(eng, b.ln[1], g)
                g = back(s, 2)
                if active(g):
                    k = parity(g)
                    eng.wait_ge(b.turned1, total(g, 1))
                    if since(g, 2):
                        eng.wait_ge(b.up, total(back(g, 2), 2))
                        eng.wait_ge(b.y2_ready, total(back(g, 2), 1))
                    eng.activation(b.hT[k], bank[2][:, :], ACT.Identity, bias=cols[:, 4:5], scale=cols[:, 3:4]).then_inc(b.h_ready, 1)
                g = back(s, 1)
                if active(g):
                    root(eng, b.ln[0], g)
                g = back(s, 7)
                if active(g):
                    eng.wait_ge(b.turned4, total(g, 1))
                    if since(g, 1):
                        eng.wait_ge(b.lr, total(back(g, 1), 2))
                    eng.activation(b.h1T, bank[6][:, :], ACT.Relu, bias=cols[:, 6:7], scale=cols[:, 5:6]).then_inc(b.h1_ready, 1)
                g = back(s, 7)
                if active(g):
                    eng.wait_ge(b.h1_ready, total(g, 1))
                    if since(g, 1):
                        eng.wait_ge(b.normed, total(back(g, 1), 1))
                    eng.activation(b.sq, b.h1T, ACT.Square).then_inc(b.squared, 1)
                g = back(s, 1)
                if active(g):
                    if since(g, 1):
                        eng.wait_ge(b.turned1, total(back(g, 1), 1))
                    normalise(eng, b.ln[0], b.y[parity(g)], b.z, g)
                g = back(s, 5)
                if active(g):
                    root(eng, b.ln[2], g)
                g = back(s, 6)
                if active(g):
                    root(eng, b.ln[3], g)
                g = back(s, 2)
                if active(g):
                    for h in range(2):
                        eng.wait_ge(b.up, part(g, 2, h + 1))
                        if since(g, 1):
                            eng.wait_ge(b.act_up, total(back(g, 1), 2))
                        eng.activation(b.small[h], bank[3 - h][:, :], ACT.Identity, bias=b1s[:, h:h + 1], scale=0.01).then_inc(b.small_up, 1)
                g = back(s, 4)
                if active(g):
                    if since(g, 1):
                        eng.wait_ge(b.y3_ready, total(back(g, 1), 3))
                    normalise(eng, b.ln[1], y2_bank[parity(g)], b.z2, g)
                g = back(s, 6)
                if active(g):
                    if since(g, 1):
                        eng.wait_ge(b.turned4, total(back(g, 1), 1))
                    normalise(eng, b.ln[3], b.x1[parity(g)], b.z4, g)
                g = back(s, 5)
                if active(g):
                    k = parity(g)
                    if since(g, 2):
                        eng.wait_ge(b.x1_out[k], slot(back(g, 2), 16))
                        eng.wait_ge(b.ln[3].applied, total(back(g, 2), LANES))
                    normalise(eng, b.ln[2], b.y3[k], b.x1[k], g)
            steps(eng, B_LAGS, b_step)
            wait_node_stores(eng)
            eng.activation(hnorm[:, :, :], hnorm[:, :, :], ACT.Sqrt).then_inc(hnorm_ready, 1)

            def c_step(s):
                g = back(s, 1)
                if active(g):
                    k = parity(g)
                    if since(g, 2):
                        eng.wait_ge(c.weighted, total(back(g, 2), 1))
                    eng.wait_ge(c.turned, part(g, 2, 1))
                    eng.activation(c.xlT[k], bank[0][:, :], ACT.Copy).then_inc(c.evacuated, 1)
                g = back(s, 2)
                if active(g):
                    k = parity(g)
                    eng.wait_ge(c.shifts, total(g, 3))
                    if since(g, 2):
                        eng.wait_ge(c.summed, total(back(g, 2), 2))
                    if since(g, 2):
                        eng.wait_ge(c.weighted, total(back(g, 2), 1))
                    eng.activation(c.pd[k], c.shift, ACT.Exp).then_inc(c.weights, 1)
                g = back(s, 3)
                if active(g):
                    k = parity(g)
                    eng.wait_ge(c.returned, part(g, 2, 1))
                    if since(g, 2):
                        eng.wait_ge(c.scattered[parity(back(g, 2))], slot(back(g, 2), 16 * LANES))
                    eng.activation(c.row[k].rearrange("p (j f) -> p j f", j=LANES)[:, :, 0:P], lanes(bank[3][:, :]), ACT.Copy).then_inc(c.packed, 1)
            steps(eng, C_LAGS, c_step)
            wait_scatters(eng, c)

            def d_step(s):
                g = back(s, 3)
                if active(g):
                    k = parity(g)
                    eng.wait_ge(d.o_ready, total(g, 1))
                    if since(g, 1):
                        eng.wait_ge(d.nrm_ready, total(back(g, 1), 1))
                    for j in range(LANES):
                        q = slice(j * P, (j + 1) * P)
                        eng.activation(d.sq[:, q], d.o2[k][:, q], ACT.Square, accum_out=d.ss[:, j:j + 1]).then_inc(d.sq_ready, 1)
                g = back(s, 3)
                if active(g):
                    eng.wait_ge(d.sq_ready, total(g, LANES))
                    if since(g, 1):
                        eng.wait_ge(d.fac_ready, total(back(g, 1), 3))
                    eng.activation(d.nrm[:, :], d.ss[:, :], ACT.Sqrt).then_inc(d.nrm_ready, 1)
                g = back(s, 4)
                if active(g):
                    root(eng, d.ln, g)
                g = back(s, 1)
                if active(g):
                    k = parity(g)
                    eng.wait_ge(d.diffs, total(g, 2))
                    if since(g, 2):
                        eng.wait_ge(d.part_e, total(back(g, 2), 1))
                        eng.wait_ge(d.part_s, total(back(g, 2), 1))
                    eng.activation(d.ex[k][:, :, :], d.diff[:, :, :], ACT.Exp).then_inc(d.exps, 1)
                g = back(s, 4)
                if active(g):
                    k = parity(g)
                    if since(g, 2):
                        eng.wait_ge(d.out_done[k], slot(back(g, 2), 16))
                    normalise(eng, d.ln, d.y[k], d.res[k], g)
            steps(eng, D_LAGS, d_step)

        @block.tensor
        def _(eng):
            eng.wait_ge(loaded, 16 * N_LOADS)
            for h in range(H0):
                eng.matmul(bank[h][:, 0:P], wq[:, h, :], wk[:, h, :], start=True, stop=True).then_inc(prep_mm, 1)
                eng.matmul(bank[2 + h][:, 0:1], wk[:, h, :], bq[:, h:h + 1], start=True, stop=True).then_inc(prep_mm, 1)
            for h in range(H0):
                mm = eng.matmul(bank[4][:, 0:ROWS_E], wq[:, h, :], wexb[:, h, :], start=h == 0, stop=h == H0 - 1)
            mm.then_inc(prep_mm, 1)
            for h in range(H0):
                mm = eng.matmul(bank[5][0:ROWS_E, 0:1], wexb[:, h, :], bq[:, h:h + 1], start=h == 0, stop=h == H0 - 1)
            mm.then_inc(prep_mm, 1)
            wait_prep(eng)

            def turn(dst, src, done):
                for j in range(LANES):
                    mm = eng.transpose(dst[:, j * P:(j + 1) * P], src[:, j * P:(j + 1) * P], ident[:, :])
                mm.then_inc(done, 1)

            def a_step(s):
                g = back(s, 4)
                if active(g):
                    k = parity(g)
                    eng.wait_ge(a.summed, total(g, 3))
                    if since(g, 1):
                        eng.wait_ge(a.combined, total(back(g, 1), LANES))
                    for j in range(LANES):
                        q = slice(j * P, (j + 1) * P)
                        o = value_bank[j]
                        if j >= 2:
                            eng.wait_ge(a.evacuated, part(within(back(s, 2)), 2, j - 1))
                        eng.matmul(o[:, 0:H0 * VCOL], a.nume[k][:, q], wve[:, :, :].rearrange("p h c -> p (h c)"), start=True, stop=False)
                        eng.matmul(o[:, 0:P], a.num[0][k][:, q], wv[:, 0, :], start=False, stop=False)
                        eng.matmul(o[:, VCOL:VCOL + P], a.num[1][k][:, q], wv[:, 1, :], start=False, stop=True).then_inc(a.values, 1)
                g = back(s, 2)
                if active(g):
                    k = parity(g)
                    eng.wait_ge(a.evacuated, total(g, 2))
                    if since(g, 1):
                        eng.wait_ge(a.products, total(back(g, 1), 3))
                    for h in range(H0):
                        eng.matmul(bank[2 + h][:, :], qk[:, h, :], a.xdT[k], start=True, stop=True).then_inc(a.projected, 1)
                    eng.matmul(bank[4][0:ROWS_E, :], qe[:, :], a.xdT[k], start=True, stop=True).then_inc(a.projected, 1)

                def spread(g, h):
                    k = parity(g)
                    if h:
                        eng.wait_ge(a.weighted, part(g, 3, h))
                    eng.matmul(bank[6][:, :], spread_w[:, h, :], a.pd[k][:, 0:W], start=True, stop=True).then_inc(a.spread, 1)
                    if h:
                        eng.wait_ge(a.summed, part(g, 3, h))
                    eng.matmul(bank[7][:, :], spread_w[:, h, :], a.pd[k][:, W:2 * W], start=True, stop=True).then_inc(a.spread, 1)
                g = back(s, 3)
                if active(g):
                    eng.wait_ge(a.weights, total(g, 1))
                    if since(g, 1):
                        eng.wait_ge(a.combined, part(back(g, 1), LANES, 2))
                    spread(g, 0)
                g = back(s, 1)
                if active(g):
                    k = parity(g)
                    eng.wait_ge(a.gathered[k], slot(g, 2 * 16 * LANES))
                    if since(g, 1):
                        eng.wait_ge(a.evacuated, total(back(g, 1), 2))
                    if since(g, 3):
                        eng.wait_ge(a.combined, total(back(g, 3), LANES))
                    turn(bank[0], a.xs[k], a.turned)
                    turn(bank[1], a.xd[k], a.turned)
                g = back(s, 3)
                if active(g):
                    spread(g, 1)
                g = back(s, 2)
                if active(g):
                    eng.wait_ge(a.products, total(g, 3))
                    if since(g, 1):
                        eng.wait_ge(a.shifts, total(back(g, 1), 3))
                    eng.matmul(bank[5][0:ROWS_E, :], sumx[:, 0, :], a.prod[0], start=True, stop=False)
                    eng.matmul(bank[5][0:ROWS_E, :], sumx[:, 1, :], a.prod[1], start=False, stop=False)
                    eng.matmul(bank[5][0:ROWS_E, :], sume[:, :], a.prode, start=False, stop=True).then_inc(a.scored, 1)
            steps(eng, A_LAGS, a_step)
            wait_scatters(eng, a)

            def b_step(s):
                g = back(s, 1)
                if active(g):
                    k = parity(g)
                    eng.wait_ge(b.node_in[k], slot(g, 48))
                    if since(g, 1):
                        eng.wait_ge(b.y_ready, total(back(g, 1), 1))
                    if since(g, 7):
                        eng.wait_ge(b.hn_saved, total(back(g, 7), 1))
                    for j in range(LANES):
                        q = slice(j * P, (j + 1) * P)
                        mm = eng.matmul(bank[1][:, q], b.xT[k][:, q], wskip[:, :], start=True, stop=True)
                    mm.then_inc(b.skipped, 1)
                g = back(s, 2)
                if active(g):
                    eng.wait_ge(b.ln[0].applied, total(g, LANES))
                    if since(g, 1):
                        eng.wait_ge(b.act_up, total(back(g, 1), 2))
                    turn(bank[2], b.z, b.turned1)
                g = back(s, 7)
                if active(g):
                    eng.wait_ge(b.ln[3].applied, total(g, LANES))
                    if since(g, 1):
                        eng.wait_ge(b.lr_ready, total(back(g, 1), 2))
                    turn(bank[6], b.z4, b.turned4)
                g = back(s, 3)
                if active(g):
                    eng.wait_ge(b.act_up, total(g, 2))
                    if since(g, 1):
                        eng.wait_ge(b.y2_ready, total(back(g, 1), 1))
                    eng.matmul(bank[4][:, :], w2[:, 0, :], b.f[0], start=True, stop=False)
                    eng.matmul(bank[4][:, :], w2[:, 1, :], b.f[1], start=False, stop=True).then_inc(b.down, 1)
                g = back(s, 2)
                if active(g):
                    k = parity(g)
                    eng.wait_ge(b.h_ready, total(g, 1))
                    if since(g, 1):
                        eng.wait_ge(b.act_up, total(back(g, 1), 2))
                    for h in range(2):
                        eng.matmul(bank[3 - h][:, :], w1[:, h, :], b.hT[k], start=True, stop=True).then_inc(b.up, 1)
                g = back(s, 7)
                if active(g):
                    eng.wait_ge(b.h1_ready, total(g, 1))
                    if since(g, 1):
                        eng.wait_ge(b.lr_ready, total(back(g, 1), 2))
                    for n in range(2):
                        for j in range(LANES):
                            q = slice(j * P, (j + 1) * P)
                            mm = eng.matmul(bank[6 + n][:, q], b.h1T[:, q], wlr[:, n, :], start=True, stop=True)
                        mm.then_inc(b.lr, 1)
                g = back(s, 7)
                if active(g):
                    eng.wait_ge(b.squared, total(g, 1))
                    if since(g, 1):
                        eng.wait_ge(b.hn_saved, total(back(g, 1), 1))
                    eng.wait_ge(b.y_ready, total(within(back(s, 1)), 1))
                    for j in range(LANES):
                        mm = eng.matmul(bank[1][:, j:j + 1], b.sq[:, j * P:(j + 1) * P], ones[:, 0:1], start=True, stop=True)
                    mm.then_inc(b.normed, 1)
                g = back(s, 3)
                if active(g):
                    eng.wait_ge(b.y2_ready, total(g, 1))
                    if since(g, 2):
                        eng.wait_ge(b.ln[1].applied, total(back(g, 2), LANES))
                    turn(y2_bank[parity(g)], b.y2T, b.turned2)
            steps(eng, B_LAGS, b_step)
            wait_node_stores(eng)

            def c_step(s):
                g = back(s, 1)
                if active(g):
                    k = parity(g)
                    eng.wait_ge(c.gathered[parity(g)], slot(g, 2 * 16 * LANES))
                    if since(g, 1):
                        eng.wait_ge(c.evacuated, total(back(g, 1), 1))
                    turn(bank[0], c.xl[k], c.turned)
                    if since(g, 1):
                        eng.wait_ge(c.feats, total(back(g, 1), 2))
                    turn(bank[1], c.xr[k], c.turned)
                g = back(s, 2)
                if active(g):
                    eng.wait_ge(c.feats, total(g, 2))
                    if since(g, 1):
                        eng.wait_ge(c.shifts, total(back(g, 1), 3))
                    eng.matmul(bank[2][:, :], attb[:, :], c.leaky, start=True, stop=True).then_inc(c.scored, 1)
                g = back(s, 3)
                if active(g):
                    k = parity(g)
                    eng.wait_ge(c.summed, total(g, 2))
                    if since(g, 1):
                        eng.wait_ge(c.packed, total(back(g, 1), 2))
                    turn(bank[3], c.num[k], c.returned)
                    for j in range(LANES):
                        q = slice(j * P, (j + 1) * P)
                        eng.matmul(bank[4][:, j * 2 * H1:j * 2 * H1 + H1], c.den[k][:, q], headpick[:, :], start=True, stop=True)
                        o = k * W + 1 + j * P
                        mm = eng.matmul(bank[4][:, j * 2 * H1 + H1:(j + 1) * 2 * H1], c.runmax[:, o:o + P], headpick[:, :], start=True, stop=True)
                    mm.then_inc(c.returned, 1)
            steps(eng, C_LAGS, c_step)


A_LAGS, B_LAGS, C_LAGS, D_LAGS = 5, 8, 4, 5


def kernel(**inputs):
    import numpy as _np
    import concourse.bacc as _bacc
    from concourse import mybir as _mybir
    from concourse.bass_utils import run_bass_kernel_spmd as _run

    v = {k: _np.asarray(a) for k, a in inputs.items()}
    l0 = {k[7:]: a for k, a in v.items() if k.startswith("L0_gnn_")}
    l1 = {k[7:]: a for k, a in v.items() if k.startswith("L1_gnn_")}
    f32 = _np.float32
    pad = NP - N_NODES
    x = _np.concatenate([v["x"], _np.zeros((pad, P), f32)])
    xT = x.reshape(BLOCKS, P, LANES, P).transpose(3, 0, 2, 1).reshape(P, NP)
    src = _np.concatenate([v["src"], _np.zeros(pad, _np.int32)])
    dst = _np.concatenate([v["dst"], _np.full(pad, N_NODES, _np.int32)])
    none = _np.full(1, NP, _np.int32)
    nxt = _np.concatenate([dst[1:], none])
    prev = _np.concatenate([none, dst[:-1]])
    idx = _np.stack([src, dst, nxt]).reshape(3, BLOCKS, LANES, P).transpose(1, 3, 0, 2)
    dstrow = _np.stack([dst.reshape(BLOCKS, W), prev.reshape(BLOCKS, W)], axis=1)
    eaT = _np.concatenate([v["edge_attr_32"], _np.zeros((pad, EDIM), f32)]).T

    head_of = _np.array([r // EDIM if r < DEN0 else r - DEN0 for r in range(ROWS_E)])
    own = (head_of[:, None] == _np.arange(H0)[None, :]).astype(f32)
    sumx = _np.broadcast_to(own.T[None], (P, H0, ROWS_E))
    sume = (head_of[:, None] == head_of[None, :]).astype(f32)
    spread_w = _np.zeros((ROWS_E, H0, P), f32)
    wexb = _np.zeros((P, H0, ROWS_E), f32)
    wve = _np.zeros((ROWS_E, H0, VCOL), f32)
    for h in range(H0):
        c = slice(h * P, (h + 1) * P)
        e = slice(h * EDIM, (h + 1) * EDIM)
        spread_w[DEN0 + h, h, :] = 1
        wexb[:, h, e] = l0["We"][c]
        wexb[:, h, DEN0 + h] = l0["bk"][c]
        wve[e, h, 0:P] = l0["We"][c].T
        wve[DEN0 + h, h, 0:P] = l0["bv"][c]
        wve[DEN0 + h, h, P] = 1
    att = l1["att"].reshape(P)
    lane = _np.arange(P)
    arrays = {
        "x": x, "xT": xT, "idx": idx, "dstrow": dstrow, "eaT": eaT,
        "ident": _np.eye(P, dtype=f32),
        "headmask": (lane[:, None] // C1 == lane[None, :] // C1).astype(f32),
        "headpick": (lane[:, None] == C1 * _np.arange(H1)[None, :]).astype(f32),
        "sumx": sumx, "sume": sume, "spread_w": spread_w,
        "Wq": l0["Wq"], "Wk": l0["Wk"], "wexb": wexb, "bq": l0["bq"].reshape(H0, P).T,
        "WvT": l0["Wv"].T, "wve": wve, "WskipT": l0["Wskip"].T, "W1T": l0["W1"].T, "W2T": l0["W2"].T,
        "W_l": l1["W_l"], "W_r": l1["W_r"],
        "cols": _np.stack([l0["b1"][:P], l0["b1"][P:], l0["b2"], l0["ln1_g"], l0["ln1_b"],
                           l1["gamma"], l1["beta"], att], axis=1),
        "rows": _np.stack([l0["bskip"], l0["ln2_g"], l0["ln2_b"], l1["b_l"], l1["b_r"], att, l1["bias"]]),
        "scale": l1["scale"].reshape(1),
    }
    arrays = {k: _np.ascontiguousarray(a) for k, a in arrays.items()}
    nc = _bacc.Bacc("TRN2", target_bir_lowering=False, num_devices=1)
    t = {k: nc.dram_tensor("in_" + k, a.shape, _mybir.dt.from_np(a.dtype), kind="ExternalInput").ap() for k, a in arrays.items()}
    out = nc.dram_tensor("out", (NP, P), F32, kind="ExternalOutput").ap()
    build(nc, t, out)
    r = _run(nc, [{"in_" + k: a for k, a in arrays.items()}], core_ids=[0])
    return r.results[0]["out"][:N_NODES]
```
